# Optimizing a Trainium2 kernel written in Bass

```python
import numpy as np
import jax
import jax.numpy as jnp

def _softmax(x, axis=-1):
    return jax.nn.softmax(x, axis=axis)

def _gelu(x):
    return jax.nn.gelu(x, approximate=True)

def _silu(x):
    return jax.nn.silu(x)

def _sigmoid(x):
    return jax.nn.sigmoid(x)

def _layernorm(x, axis=-1, eps=1e-05):
    m = jnp.mean(x, axis=axis, keepdims=True)
    v = jnp.var(x, axis=axis, keepdims=True)
    return (x - m) / jnp.sqrt(v + eps)

def _scatter_add(tgt, idx, src, axis=0):
    return tgt.at[idx].add(src)

def _segment_sum(src, seg, n):
    return jax.ops.segment_sum(src, seg, n)
kernel_name = 'mk_gnn_preln_d2_gnn_r8_886263'

def setup_inputs(seed: int=0):
    np.random.seed(seed)
    _w = jnp.asarray

    def _rec_inputs():
        import jax
        import jax.numpy as jnp
        _gk = jax.random.key(seed)
        x = -0.000202 + 1 * jax.random.normal(jax.random.fold_in(_gk, 1), (12500, 64), jnp.float32)
        _s = jax.random.randint(jax.random.fold_in(_gk, 2), (200000,), 0, 12500, jnp.int32)
        _d = jax.random.randint(jax.random.fold_in(_gk, 3), (200000,), 0, 12500, jnp.int32)
        _loop = jnp.arange(12500, dtype=jnp.int32)
        src = jnp.concatenate([_s, _d, _loop])
        dst = jnp.concatenate([_d, _s, _loop])
        _o = jnp.argsort(dst, stable=True)
        src = src[_o]
        dst = dst[_o]
        edge_weight1 = jax.random.uniform(jax.random.fold_in(_gk, 13), (412500, 1), jnp.float32, 0.0, 0.999999)
        return (x, src, dst, edge_weight1)
    x, src, dst, edge_weight1 = _rec_inputs()

    def _L0_gnn_setup():
        import jax, jax.numpy as jnp
        import numpy as np
        N_NODES = 12500

        def _sage_pool_layer(x, src, dst, W_pool, b_pool, W_self, W_neigh, bias):
            m = jax.nn.relu(x[src] @ W_pool + b_pool)
            agg = jax.ops.segment_max(m, dst, num_segments=N_NODES)
            agg = jnp.where(jnp.isfinite(agg), agg, jnp.zeros((), x.dtype))
            return x @ W_self + agg @ W_neigh + bias
        key = jax.random.key(seed)
        ks = jax.random.split(key, 13)
        d = 64
        E = 200000
        s = 1.0 / np.sqrt(d)
        inp = {'x': jax.random.normal(ks[0], (N_NODES, d), jnp.float32), 'edge_src': jax.random.randint(ks[1], (E,), 0, N_NODES, jnp.int32), 'edge_dst': jax.random.randint(ks[2], (E,), 0, N_NODES, jnp.int32)}
        names = ['W_pool1', 'b_pool1', 'W_self1', 'W_neigh1', 'bias1', 'W_pool2', 'b_pool2', 'W_self2', 'W_neigh2', 'bias2']
        shapes = [(d, d), (d,), (d, d), (d, d), (d,)] * 2
        for name, shp, k in zip(names, shapes, ks[3:]):
            inp[name] = jax.random.uniform(k, shp, jnp.float32, -s, s)
        return inp
    _L0_gnn_all = _L0_gnn_setup()
    _L0_gnn_in = {k: v for k, v in _L0_gnn_all.items() if k in ('W_pool1', 'b_pool1', 'W_self1', 'W_neigh1', 'bias1', 'W_pool2', 'b_pool2', 'W_self2', 'W_neigh2', 'bias2')}
    del _L0_gnn_all

    def _L1_gnn_setup():
        import jax, jax.numpy as jnp
        import numpy as np
        N_NODES = 12500
        N_EDGES = 200000
        HID = 64
        N_LAYERS = 3
        BN_EPS = 1e-05
        key = jax.random.key(seed)
        ks = jax.random.split(key, 10)
        x = jax.random.normal(ks[0], (N_NODES, HID), dtype=jnp.float32)
        edge_index = jax.random.randint(ks[1], (2, N_EDGES), 0, N_NODES, dtype=jnp.int64)
        edge_atten = jax.random.uniform(ks[2], (N_EDGES, 1), dtype=jnp.float32)
        s = 1.0 / np.sqrt(HID)
        W1 = jax.random.normal(ks[3], (N_LAYERS, HID, HID), dtype=jnp.float32) * s
        b1 = jax.random.normal(ks[4], (N_LAYERS, HID), dtype=jnp.float32) * s
        gamma = jnp.ones((N_LAYERS, HID), dtype=jnp.float32)
        beta = jnp.zeros((N_LAYERS, HID), dtype=jnp.float32)
        W2 = jax.random.normal(ks[5], (N_LAYERS, HID, HID), dtype=jnp.float32) * s
        b2 = jax.random.normal(ks[6], (N_LAYERS, HID), dtype=jnp.float32) * s
        return {'x': x, 'edge_index': edge_index, 'edge_atten': edge_atten, 'W1': W1, 'b1': b1, 'gamma': gamma, 'beta': beta, 'W2': W2, 'b2': b2}
    _L1_gnn_all = _L1_gnn_setup()
    _L1_gnn_in = {k: v for k, v in _L1_gnn_all.items() if k in ('W1', 'b1', 'gamma', 'beta', 'W2', 'b2')}
    del _L1_gnn_all
    return {'x': x, 'src': src, 'dst': dst, 'edge_weight1': edge_weight1, 'L0_gnn_W_pool1': _L0_gnn_in['W_pool1'], 'L0_gnn_b_pool1': _L0_gnn_in['b_pool1'], 'L0_gnn_W_self1': _L0_gnn_in['W_self1'], 'L0_gnn_W_neigh1': _L0_gnn_in['W_neigh1'], 'L0_gnn_bias1': _L0_gnn_in['bias1'], 'L0_gnn_W_pool2': _L0_gnn_in['W_pool2'], 'L0_gnn_b_pool2': _L0_gnn_in['b_pool2'], 'L0_gnn_W_self2': _L0_gnn_in['W_self2'], 'L0_gnn_W_neigh2': _L0_gnn_in['W_neigh2'], 'L0_gnn_bias2': _L0_gnn_in['bias2'], 'L1_gnn_W1': _L1_gnn_in['W1'], 'L1_gnn_b1': _L1_gnn_in['b1'], 'L1_gnn_gamma': _L1_gnn_in['gamma'], 'L1_gnn_beta': _L1_gnn_in['beta'], 'L1_gnn_W2': _L1_gnn_in['W2'], 'L1_gnn_b2': _L1_gnn_in['b2']}

def reference(x, src, dst, edge_weight1, L0_gnn_W_pool1, L0_gnn_b_pool1, L0_gnn_W_self1, L0_gnn_W_neigh1, L0_gnn_bias1, L0_gnn_W_pool2, L0_gnn_b_pool2, L0_gnn_W_self2, L0_gnn_W_neigh2, L0_gnn_bias2, L1_gnn_W1, L1_gnn_b1, L1_gnn_gamma, L1_gnn_beta, L1_gnn_W2, L1_gnn_b2):
    import jax
    import jax.numpy as jnp

    def _L0_gnn_ref(x, edge_src, edge_dst, W_pool1, b_pool1, W_self1, W_neigh1, bias1, W_pool2, b_pool2, W_self2, W_neigh2, bias2):
        import jax, jax.numpy as jnp
        import numpy as np
        N_NODES = 12500

        def _sage_pool_layer(x, src, dst, W_pool, b_pool, W_self, W_neigh, bias):
            m = jax.nn.relu(x[src] @ W_pool + b_pool)
            agg = jax.ops.segment_max(m, dst, num_segments=N_NODES)
            agg = jnp.where(jnp.isfinite(agg), agg, jnp.zeros((), x.dtype))
            return x @ W_self + agg @ W_neigh + bias
        h = _sage_pool_layer(x, edge_src, edge_dst, W_pool1, b_pool1, W_self1, W_neigh1, bias1)
        h = jnp.tanh(h)
        h = _sage_pool_layer(h, edge_src, edge_dst, W_pool2, b_pool2, W_self2, W_neigh2, bias2)
        return h

    def _L1_gnn_ref(x, edge_index, edge_atten, W1, b1, gamma, beta, W2, b2):
        import jax, jax.numpy as jnp
        import numpy as np
        N_NODES = 12500
        N_EDGES = 200000
        HID = 64
        N_LAYERS = 3
        BN_EPS = 1e-05
        src = edge_index[0]
        dst = edge_index[1]
        n = x.shape[0]
        for i in range(N_LAYERS):
            msg = x[src] * edge_atten
            agg = jax.ops.segment_sum(msg, dst, num_segments=n)
            h = agg + x
            h = h @ W1[i] + b1[i]
            mu = jnp.mean(h, axis=0)
            var = jnp.var(h, axis=0)
            h = (h - mu) * jax.lax.rsqrt(var + BN_EPS) * gamma[i] + beta[i]
            h = jax.nn.relu(h)
            h = h @ W2[i] + b2[i]
            x = jax.nn.relu(h)
        return x
    edge_index = jnp.stack([src, dst])
    h = jnp.maximum(_layernorm(x, axis=-1), 0.0)
    x = x + _L0_gnn_ref(h, src, dst, L0_gnn_W_pool1, L0_gnn_b_pool1, L0_gnn_W_self1, L0_gnn_W_neigh1, L0_gnn_bias1, L0_gnn_W_pool2, L0_gnn_b_pool2, L0_gnn_W_self2, L0_gnn_W_neigh2, L0_gnn_bias2)
    h = jnp.maximum(_layernorm(x, axis=-1), 0.0)
    x = x + _L1_gnn_ref(h, edge_index, edge_weight1, L1_gnn_W1, L1_gnn_b1, L1_gnn_gamma, L1_gnn_beta, L1_gnn_W2, L1_gnn_b2)
    return x

_drawn_inputs = setup_inputs


def setup_inputs(seed=0):
    import zlib

    import numpy as np

    out = dict(_drawn_inputs(seed))
    spreads = {'L1_gnn_gamma': (1.0, 0.2), 'L1_gnn_beta': (0.0, 0.1)}
    factors = {'L0_gnn_b_pool1': 3.059, 'L1_gnn_b1': 8.0}
    for name, (base, spread) in spreads.items():
        noise = np.random.default_rng([zlib.crc32(name.encode()), seed]).standard_normal(out[name].shape)
        drawn = base * np.exp(spread * noise) if base else spread * noise
        out[name] = jnp.asarray(drawn.astype(out[name].dtype))
    for name, factor in factors.items():
        out[name] = (out[name] * factor).astype(out[name].dtype)
    return out
```

```python
from contextlib import ExitStack

import numpy as np
import concourse.bass as bass
from concourse import mybir

N, D, E = 12500, 64, 412500
P = 128
NT = -(-N // P)
LAST_ROWS = N - (P - 1) * NT
PAIRS = NT // 2
PER_GROUP = 4
NG = -(-PAIRS // PER_GROUP)
GROUPS = [(PER_GROUP * g, min(PAIRS, PER_GROUP * (g + 1))) for g in range(NG)]

SLOTS, SLOT_STEPS = 4, 13
TURN = SLOTS * SLOT_STEPS
HALF = TURN // 2
A, B = 0, 1
TURNS = (26, 36)
STEPS_A, STEPS_B = (t * TURN for t in TURNS)
REGION_STEPS = (STEPS_A, STEPS_B)
STEPS = STEPS_A + STEPS_B
PADS = P * STEPS - E
EDGES_A = P * STEPS_A - PADS
FIRST_ROW = (0, P * STEPS_A)
FIRST_COL = (0, STEPS_A)
ZERO_ROW = P * STEPS
assert 0 <= PADS < STEPS_A

DENSE_P = 54
DENSE = DENSE_P * NT
DENSE_SHIFT = 2
CHUNK_TILES = 14
CHUNK = CHUNK_TILES * DENSE_P
CHUNKS = NT // CHUNK_TILES
HALF_CHUNK = CHUNK // 2
DENSE_TILES = 2
SCATTERS = 13
MAX_DEGREE = STEPS_A // SCATTERS
SCATTER_GROUPS = (0, 4, 7, 10, 13)
PASSES = 5
MAX_PASSES = 2

ROW = 625
E_ROWS = E // ROW
HALF_SAMPLES = E_ROWS // 2
SEARCH_SLOTS = 4
SEARCH_TILES = 3
SEARCH_TURNS = (NT + 1) // SEARCH_TILES
assert SEARCH_TILES * SEARCH_TURNS == NT + 1 and SEARCH_TURNS < TURNS[B]
LN_EPS = BN_EPS = 1e-5


def build(nc, io):
    F32, I32 = mybir.dt.float32, mybir.dt.int32
    ALU, ACT, AX = mybir.AluOpType, mybir.ActivationFunctionType, mybir.AxisListType
    ctx = ExitStack()
    with ctx:
        def sb(name, shape, dt=F32):
            return ctx.enter_context(nc.sbuf_tensor(name, shape, dt))

        def ps(name):
            return ctx.enter_context(nc.psum_tensor(name, [P, 512], F32))

        def sem(name):
            return ctx.enter_context(nc.semaphore(name))

        table = nc.dram_tensor("table", [P * NT, D], F32, kind="Internal").ap()
        states = nc.dram_tensor("states", [P * STEPS + 1, D], F32, kind="Internal").ap()
        table_rows = table.rearrange("(p t) f -> p (t f)", p=P)
        states_rows = [states[FIRST_ROW[r]:FIRST_ROW[r] + P * REGION_STEPS[r], :].rearrange("(p j) f -> p (j f)", p=P)
                       for r in (A, B)]
        adjacency = nc.dram_tensor("adjacency", [P * NT * DENSE, 1], F32, kind="Internal").ap()
        adjacency_rows = adjacency.rearrange("(p c) a -> p (c a)", p=P)
        dst_rows = io["dst"].rearrange("(r c) -> r c", c=ROW)

        x_res = sb("x_res", [P, NT * D])
        node = sb("node", [P, NT * D])
        agg = sb("agg", [P, NT * D])
        feat_all = sb("feat", [P, max(PAIRS * P, CHUNKS * CHUNK)])
        feat = feat_all[:, 0:PAIRS * P]
        chunk = feat_all[:, 0:CHUNKS * CHUNK].rearrange("p (c n) -> p c n", n=CHUNK)
        x_tile = sb("x_tile", [P, DENSE_TILES, D])
        zeros = sb("zeros", [P, HALF_CHUNK])
        src = sb("src", [P, STEPS], I32)
        same = sb("same", [P, STEPS])
        weight = sb("weight", [P, STEPS])
        dst = sb("dst_sb", [P, STEPS + 2], I32)
        dst_at = [dst[:, 0:STEPS_A + 1], dst[:, STEPS_A + 1:]]
        scatter_idx = dst[:, 1:STEPS_A + 1]
        idx_st = sb("idx_st", [P, TURN], I32)
        same_st = sb("same_st", [P, TURN])
        weight_st = sb("weight_st", [P, TURN])
        rows = sb("rows", [P, SLOTS, SLOT_STEPS, D])
        state = sb("state", [P, SLOTS, SLOT_STEPS, D])
        samples = agg[:, 0:E_ROWS]
        sample_i = agg[0:1, NT * D - E_ROWS:].bitcast(I32)
        sample_f = agg[0:1, NT * D - 2 * E_ROWS:NT * D - E_ROWS]
        nval_i = sb("nval_i", [P, NT + 1], I32)
        nval = sb("nval", [P, NT + 1])
        cnt_rows = sb("cnt_rows", [P, NT + 1])
        row_idx = sb("row_idx", [P, NT + 1], I32)
        cnt_in = sb("cnt_in", [P, NT + 1])
        cnt = sb("cnt", [P, NT + 1])
        some = sb("some", [P, NT])
        ends_f = sb("ends_f", [P, NT])
        ends = sb("ends", [P, NT], I32)
        ends_b = sb("ends_b", [P, NT], I32)
        in_b = sb("in_b", [P, NT])
        guard = sb("guard", [P, 2])
        guard_row = sb("guard_row", [1, 2 * P])
        dense_f = sb("dense_f", [P, 1])
        general_f = sb("general_f", [1, 1])
        general_i = sb("general_i", [1, 1], I32)
        lead_flags = agg[:, 0:max(REGION_STEPS)]
        lead = sb("lead", [P, 2])
        cont = sb("cont", [P, 2])
        whole = sb("whole", [P, 2])
        fix_f = sb("fix_f", [P, 2])
        base_i = sb("base_i", [P, 2], I32)
        fix_row = sb("fix_row", [P, 2], I32)
        whole_t = sb("whole_t", [D, 2, P])
        carry = sb("carry", [D, 2, P + 1])
        finals = sb("finals", [P, 2, D])
        fixed_rows = sb("fixed_rows", [P, 2, D])
        search_i = agg[:, 0:SEARCH_SLOTS * ROW].bitcast(I32).rearrange("p (s c) -> p s c", c=ROW)
        search_f = agg[:, SEARCH_SLOTS * ROW:2 * SEARCH_SLOTS * ROW].rearrange("p (s c) -> p s c", c=ROW)
        row_flags = agg[:, E_ROWS:2 * E_ROWS]
        search_flags = agg[:, 2 * SEARCH_SLOTS * ROW:(2 * SEARCH_SLOTS + 1) * ROW]
        idx_hi = agg[:, 0:STEPS_A].bitcast(I32)
        t_part = agg[:, STEPS_A:2 * STEPS_A]
        agg_t = sb("agg_t", [P, 2, 512])
        ident = sb("ident", [P, P])
        ones = sb("ones", [1, P])
        stat = sb("stat", [P, 4, NT])
        layer_norm = state[:, :, :, :].rearrange("p s j f -> p (s j f)")
        centred = layer_norm[:, 0:512]
        squares = layer_norm[:, 512:1024]
        bn = sb("bn", [P, PAIRS, 6])
        bn_mv = sb("bn_mv", [P, 2])
        bn_mean = sb("bn_mean", [P, 1])
        bn_dev = sb("bn_dev", [P, 1])
        bn_var = sb("bn_var", [P, 1])
        bn_std = sb("bn_std", [P, 1])
        bn_scale = sb("bn_scale", [P, 1])
        bn_shift = sb("bn_shift", [P, 1])
        fold = sb("fold", [P, P])
        W_NAMES = ["pool1", "self1", "neigh1", "pool2", "self2", "neigh2"] + \
            [f"w1_{i}" for i in range(3)] + [f"w2_{i}" for i in range(3)]
        W_FROM = [io["L0_gnn_W_pool1"], io["L0_gnn_W_self1"], io["L0_gnn_W_neigh1"],
                  io["L0_gnn_W_pool2"], io["L0_gnn_W_self2"], io["L0_gnn_W_neigh2"]] + \
            [io["L1_gnn_W1"][i] for i in range(3)] + [io["L1_gnn_W2"][i] for i in range(3)]
        w_all = sb("w_all", [P, len(W_NAMES), P])
        W = {n: w_all[:, i, :] for i, n in enumerate(W_NAMES)}
        ROWS_FROM = [("pool1", io["L0_gnn_b_pool1"]), ("pool2", io["L0_gnn_b_pool2"]),
                     ("out2", io["L0_gnn_bias2"])] + [(f"b2_{i}", io["L1_gnn_b2"][i]) for i in range(3)]
        BF16 = mybir.dt.bfloat16
        PART_AT = (0, 32, 64)
        PARTS = PART_AT[-1] + 1
        BIASES = len(ROWS_FROM) * D
        bias_parts = sb("bias_parts", [PARTS, BIASES], BF16)
        B_ROW = {n: bias_parts[:, None, i * D:(i + 1) * D] for i, (n, _) in enumerate(ROWS_FROM)}
        bias_ones = sb("bias_ones", [PARTS, P], BF16)
        set_up = state[0:PARTS, :, :, :].rearrange("p s j f -> p (s j f)")
        bias_f, bias_rest = set_up[:, 0:BIASES], set_up[:, BIASES:2 * BIASES]
        bias_split = [set_up[:, 2 * BIASES + n * (BIASES // 2):2 * BIASES + (n + 1) * (BIASES // 2)].bitcast(BF16)
                      for n in range(len(PART_AT))]
        COLS_FROM = [("out1", io["L0_gnn_bias1"])] + [(f"{a}_{i}", io[b][i]) for i in range(3) for a, b in
                     (("b1", "L1_gnn_b1"), ("gamma", "L1_gnn_gamma"), ("beta", "L1_gnn_beta"))]
        cols = sb("cols", [P, len(COLS_FROM)])
        COL = {n: cols[:, i:i + 1] for i, (n, _) in enumerate(COLS_FROM)}

        PARAMS = 16 * (2 * len(W_FROM) + 2 * len(COLS_FROM))

        ps_t = [ps("ps_t0"), ps("ps_t1")]
        ps_f = [ps("ps_f0"), ps("ps_f1")]
        ps_m = [ps("ps_m0"), ps("ps_m1")]
        ps_tail = ps("ps_tail")
        ps_carry = [ps_tail[:, 2 * P + r * D:2 * P + (r + 1) * D] for r in (A, B)]
        ps_bn = ps_tail[:, 2 * P + 2 * D:2 * P + 2 * D + 2]
        ps_dense = [*ps_t, *ps_f, *ps_m, ps("ps_dense6")]

        zeroed = sem("zeroed")
        x_in = sem("x_in")
        edges_in = sem("edges_in")
        weights_in = sem("weights_in")
        params_in = sem("params_in")
        biases_in = sem("biases_in")
        biases_ready = sem("biases_ready")
        consts = sem("consts")
        sample_in = sem("sample_in")
        sample_ready = sem("sample_ready")
        own = sem("own")
        same_ready = sem("same_ready")
        lead_ready = sem("lead_ready")
        guard_ready = sem("guard_ready")
        guard_ps = sem("guard_ps")
        flag_ready = sem("flag_ready")
        ln_centred = sem("ln_centred")
        ln_squared = sem("ln_squared")
        ln_var = sem("ln_var")
        ln_root = sem("ln_root")
        ln_ready = sem("ln_ready")
        samples_ps = sem("samples_ps")
        tile_counted = sem("tile_counted")
        whole_ps = sem("whole_ps")
        row_wanted = sem("row_wanted")
        row_in = [sem(f"row_in{s}") for s in range(SEARCH_SLOTS)]
        row_f = sem("row_f")
        row_counted = sem("row_counted")
        ends_ready = sem("ends_ready")
        table_in = sem("table_in")
        idx_staged = [sem(f"idx_staged{r}") for r in "AB"]
        same_staged = [sem(f"same_staged{r}") for r in "AB"]
        weight_staged = [sem(f"weight_staged{r}") for r in "AB"]
        gathered = [[sem(f"gathered{k}_{s}") for s in range(SLOTS)] for k in range(PASSES)]
        weighted = [sem(f"weighted{r}") for r in "AB"]
        step_done = [sem(f"step_done{r}") for r in "AB"]
        stored = [[sem(f"stored{r}{s}") for s in range(SLOTS)] for r in "AB"]
        final_ready = [sem(f"final_ready{r}") for r in "AB"]
        tail_t = [sem(f"tail_t{r}") for r in "AB"]
        carry_set = sem("carry_set")
        carried = [sem(f"carried{r}") for r in "AB"]
        carry_t = [sem(f"carry_t{r}") for r in "AB"]
        fix_in = [sem(f"fix_in{r}") for r in "AB"]
        fixed = [sem(f"fixed{r}") for r in "AB"]
        fix_out = [sem(f"fix_out{r}") for r in "AB"]
        cleared = sem("cleared")
        cols_ready = sem("cols_ready")
        elems_ready = sem("elems_ready")
        sweep_staged = sem("sweep_staged")
        scattered = [[sem(f"scattered{u}_{g}") for g in range(4)] for u in range(2)]
        x_tile_in = [sem(f"x_tile_in{u}") for u in range(DENSE_TILES)]
        chunk_in = [sem(f"chunk_in{c}") for c in range(CHUNKS)]
        chunk_used = sem("chunk_used")
        dense_out = sem("dense_out")
        dense_added = sem("dense_added")
        agg_in = [sem(f"agg_in{g}") for g in range(NG)]
        summed = sem("summed")
        transposed = sem("transposed")
        copied = sem("copied")
        mixed = sem("mixed")
        activated = sem("activated")
        bn_in = sem("bn_in")
        bn_ps = sem("bn_ps")
        bn_root = sem("bn_root")
        bn_ready = sem("bn_ready")
        normed = sem("normed")
        projected = sem("projected")
        emitted = sem("emitted")
        out_in = sem("out_in")
        IN_PHASES = {"summed": (3, 4, 5), "transposed": range(6), "copied": range(6),
                     "mixed": (1, 3, 4, 5), "activated": (1, 3, 4, 5), "normed": (3, 4, 5),
                     "projected": range(6), "emitted": range(6)}

        def nth(event, phase, g):
            return NG * list(IN_PHASES[event]).index(phase) + g + 1

        def agg_landed(k, g):
            return 16 * 2 * (GROUPS[g][1] - GROUPS[g][0]) * (k + 1)

        def span(g):
            a, b = GROUPS[g]
            return slice(a * P, b * P)

        def by_tile(ap):
            return ap.rearrange("p (t f) -> p t f", f=D)

        def flag(engine):
            engine.wait_ge(flag_ready, 1)
            return engine.value_load(general_i[0:1, 0:1], min_val=0, max_val=1)

        def tiles_of(ap):
            return ap.rearrange("p (q n) -> p q n", n=P)[:, :, 0:DENSE_P]

        SWEEP_PAIRS = MAX_DEGREE // 2
        GROUP_SCATTERS = [b - a for a, b in zip(SCATTER_GROUPS, SCATTER_GROUPS[1:])]

        block = ctx.enter_context(nc.Block())
        TABLE_DMAS = NG

        @block.sync
        def _(sp):
            x_rows = io["x"][0:(P - 1) * NT, :].rearrange("(p t) f -> p (t f)", t=NT)
            sp.wait_ge(zeroed, 1)
            sp.dma_start(x_res[0:112, :], x_rows[0:112, :]).then_inc(x_in, 16)
            sp.dma_start(x_res[112:P - 1, :], x_rows[112:P - 1, :]).then_inc(x_in, 16)
            sp.dma_start(x_res[P - 1:P, 0:LAST_ROWS * D],
                         io["x"][(P - 1) * NT:N, :].rearrange("(p t) f -> p (t f)", p=1)).then_inc(x_in, 16)
            sp.dma_start(sample_i, io["dst"].rearrange("(r c) -> c r", c=ROW)[ROW - 1:ROW, :],
                         allow_slow_non_contiguous=True).then_inc(sample_in, 16)
            sp.wait_ge(zeroed, 4)
            FIRST = STEPS_A - PADS

            def load_edges(to_a, to_b, name, done):
                rest = io[name][FIRST:EDGES_A].rearrange("(p j) -> p j", j=STEPS_A)
                sp.dma_start(to_a[0:1, PADS:STEPS_A],
                             io[name][0:FIRST].rearrange("(p j) -> p j", p=1)).then_inc(done, 16)
                sp.dma_start(to_a[1:113, :], rest[0:112, :]).then_inc(done, 16)
                sp.dma_start(to_a[113:P, :], rest[112:P - 1, :]).then_inc(done, 16)
                sp.dma_start(to_b, io[name][EDGES_A:E].rearrange("(p j) -> p j", j=STEPS_B)).then_inc(done, 16)

            load_edges(dst_at[A][:, 1:], dst_at[B][:, 1:], "dst", edges_in)
            for to, first, steps in ((dst_at[A][1:P, 0:1], FIRST - 1, STEPS_A), (dst_at[B][:, 0:1], EDGES_A - 1, STEPS_B)):
                n = to.shape[0]
                sp.dma_start(to, io["dst"][first:first + (n - 1) * steps + 1:steps].rearrange("(p a) -> p a", a=1),
                             allow_slow_non_contiguous=True).then_inc(edges_in, 16)
            load_edges(src[:, 0:STEPS_A], src[:, STEPS_A:], "src", edges_in)
            load_edges(weight[:, 0:STEPS_A], weight[:, STEPS_A:], "edge_weight1", weights_in)
            sp.wait_ge(zeroed, 5)
            sp.dma_start(states[ZERO_ROW:ZERO_ROW + 1, :], zeros[0:1, 0:D]).then_inc(weights_in, 16)

            def store_table(phase):
                for g in range(NG):
                    sp.wait_ge(emitted, nth("emitted", phase, g))
                    sp.dma_start(table_rows[:, span(g)], node[:, span(g)]).then_inc(table_in, 16)

            def clear_tile(at):
                sp.dma_start(adjacency_rows[:, bass.ds(at, DENSE)].rearrange("p (c n) -> p c n", n=HALF_CHUNK),
                             zeros[:, None, :].broadcast_to([P, DENSE // HALF_CHUNK, HALF_CHUNK])).then_inc(cleared, 16)

            for k in range(PASSES):
                store_table(k)
                if k == MAX_PASSES:
                    general = flag(sp)
                if k == 0:
                    with sp.Fori(0, NT // 2 // 2) as i:
                        at = [sp.snap(i * (2 * DENSE) + u * DENSE) for u in range(2)]
                        sp.wait_ge(step_done[B], i * TURN + TURN)
                        for u in range(2):
                            clear_tile(at[u])
                elif k == 1:
                    with sp.Fori(0, NT // 2 - NT // 2 // 2) as i:
                        at = [sp.snap(i * (2 * DENSE) + (2 * (NT // 2 // 2) + u) * DENSE) for u in range(2)]
                        sp.wait_ge(step_done[B], i * TURN + (STEPS_B + TURN))
                        for u in range(2):
                            clear_tile(at[u])
                else:
                    with sp.If(general == 0):
                        base = (k - MAX_PASSES) * NT
                        sp.wait_ge(table_in, 16 * TABLE_DMAS * (k + 1))
                        if k == MAX_PASSES:
                            for u in range(2):
                                for g, n in enumerate(GROUP_SCATTERS):
                                    sp.wait_ge(scattered[u][g], 16 * n * SWEEP_PAIRS)

                        def stream(turn, first):
                            for u in range(DENSE_TILES):
                                rows_at = sp.snap(turn * (DENSE_TILES * D) + u * D)
                                for c in range(CHUNKS):
                                    at = sp.snap(turn * (DENSE_TILES * DENSE) + (u * DENSE + c * CHUNK))
                                    if not (first and u == 0):
                                        sp.wait_ge(chunk_used, turn * (DENSE_TILES * CHUNKS) +
                                                   (base * CHUNKS + (u - 1) * CHUNKS + c + 1))
                                    if c == 0:
                                        sp.dma_start(x_tile[:, u, :], table_rows[:, bass.ds(rows_at, D)]
                                                     ).then_inc(x_tile_in[u], 16)
                                    sp.dma_start(chunk[:, c, :], adjacency_rows[:, bass.ds(at, CHUNK)]).then_inc(chunk_in[c], 16)

                        stream(0, True)
                        with sp.Fori(1, NT // DENSE_TILES) as turn:
                            stream(turn, False)
                    sp.nop()

            out_rows = io["out"][0:(P - 1) * NT, :].rearrange("(p t) f -> p (t f)", t=NT)
            for g in range(NG):
                sp.wait_ge(emitted, nth("emitted", PASSES, g))
                sp.dma_start(out_rows[0:112, span(g)], node[0:112, span(g)]).then_inc(out_in, 16)
                sp.dma_start(out_rows[112:P - 1, span(g)], node[112:P - 1, span(g)]).then_inc(out_in, 16)
            sp.dma_start(io["out"][(P - 1) * NT:N, :].rearrange("(p t) f -> p (t f)", p=1),
                         node[P - 1:P, 0:LAST_ROWS * D]).then_inc(out_in, 16)
            sp.wait_ge(out_in, 16 * (2 * NG + 1))

        @block.gpsimd
        def _(pool):
            pool.memset(ident[:, :], 0.0).then_inc(consts, 1)
            pool.memset(fold[:, :], 0.0).then_inc(consts, 1)
            pool.iota(nval_i[:, :], pattern=[[1, NT + 1]], base=-1, channel_multiplier=NT).then_inc(consts, 1)
            pool.iota(base_i[:, 0:1], pattern=[[0, 1]], base=FIRST_ROW[A], channel_multiplier=STEPS_A).then_inc(consts, 1)
            pool.iota(base_i[:, 1:2], pattern=[[0, 1]], base=FIRST_ROW[B], channel_multiplier=STEPS_B).then_inc(consts, 1)
            pool.wait_ge(consts, 5)
            pool.affine_select(out=ident[:, :], in_=ident[:, :], compare_op=ALU.not_equal, fill=1.0,
                               base=0, pattern=[[-1, P]], channel_multiplier=1).then_inc(consts, 1)
            for n, off in enumerate((0, D, -D)):
                pool.affine_select(out=fold[:, :], in_=fold[:, :], compare_op=ALU.not_equal, fill=0.5,
                                   base=off, pattern=[[-1, P]], channel_multiplier=1).then_inc(consts, 1)
                pool.wait_ge(consts, 7 + n)

            staged_next = ctx.enter_context(pool.register("staged_next"))
            scattered_next = [[ctx.enter_context(pool.register(f"scattered_next{u}_{g}")) for g in range(4)]
                              for u in range(2)]

            def gather_search():
                pool.wait_ge(row_wanted, 1)
                for t in range(NT + 1):
                    s = t % SEARCH_SLOTS
                    if t >= SEARCH_SLOTS:
                        pool.wait_ge(row_f, t - SEARCH_SLOTS + 1)
                    pool.indirect_dma_start(
                        out=search_i[:, s, :], out_offset=None, in_=dst_rows,
                        in_offset=bass.IndirectOffsetOnAxis(ap=row_idx[:, t:t + 1], axis=0)).then_inc(row_in[s], 16)

            def gather_region(k, r):
                pool.reg_mov(staged_next, k * 2 * TURNS[r] + 1)

                def gather_turn():
                    for half in range(2):
                        pool.wait_ge(idx_staged[r], staged_next)
                        pool.reg_add(staged_next, staged_next, 1)
                        pool.wait_ge(table_in, 16 * TABLE_DMAS * (k + 1))
                        for j in range(half * HALF, (half + 1) * HALF):
                            s, i = divmod(j, SLOT_STEPS)
                            pool.indirect_dma_start(
                                out=rows[:, s, i, :], out_offset=None, in_=table,
                                in_offset=bass.IndirectOffsetOnAxis(ap=idx_st[:, j:j + 1], axis=0),
                            ).then_inc(gathered[k][s], 16)

                with pool.Fori(0, TURNS[r]) as turn:
                    gather_turn()

            def fix_region(k, r):
                for s in range(SLOTS):
                    pool.wait_ge(stored[r][s], 16 * TURNS[r] * (k + 1))
                fix_at = bass.IndirectOffsetOnAxis(ap=fix_row[:, r:r + 1], axis=0)
                pool.indirect_dma_start(out=fixed_rows[:, r, :], out_offset=None, in_=states,
                                        in_offset=fix_at).then_inc(fix_in[r], 16)
                pool.wait_ge(fixed[r], k + 1)
                pool.indirect_dma_start(out=states, out_offset=fix_at, in_=fixed_rows[:, r, :],
                                        in_offset=None).then_inc(fix_out[r], 16)
                pool.wait_ge(fix_out[r], 16 * (k + 1))

            def finish_elements():
                pool.wait_ge(cols_ready, 2)
                pool.tensor_tensor(scatter_idx, idx_hi, scatter_idx, ALU.add).then_inc(elems_ready, 1)
                pool.wait_ge(elems_ready, 1)
                pool.iota(scatter_idx[0:1, 0:PADS], pattern=[[1, PADS]], base=N * DENSE,
                          channel_multiplier=0).then_inc(elems_ready, 1)

            def scatter_adjacency():
                pool.wait_ge(cleared, 16 * NT)
                pool.reg_mov(staged_next, 2)
                for row in scattered_next:
                    for g, register in enumerate(row):
                        pool.reg_mov(register, 16 * GROUP_SCATTERS[g])

                def wait_landed(u, g):
                    pool.wait_ge(scattered[u][g], scattered_next[u][g])
                    pool.reg_add(scattered_next[u][g], scattered_next[u][g], 16 * GROUP_SCATTERS[g])

                def sweep_pair(first):
                    for u in range(2):
                        pool.wait_ge(sweep_staged, staged_next)
                        pool.reg_add(staged_next, staged_next, 2)
                        for g, n in enumerate(GROUP_SCATTERS):
                            if g == 3:
                                wait_landed(u, 0)
                            elif u == 1:
                                wait_landed(0, g + 1)
                            elif not first:
                                wait_landed(1, g + 1)
                            for c in range(SCATTER_GROUPS[g], SCATTER_GROUPS[g + 1]):
                                at = u * SCATTERS + c
                                pool.indirect_dma_start(
                                    out=adjacency, in_=weight_st[:, at:at + 1], in_offset=None, compute_op=ALU.add,
                                    out_offset=bass.IndirectOffsetOnAxis(ap=idx_st[:, at:at + 1], axis=0),
                                ).then_inc(scattered[u][g], 16)

                sweep_pair(True)
                with pool.Fori(1, SWEEP_PAIRS) as pair:
                    sweep_pair(False)
                for u in range(2):
                    for g, n in enumerate(GROUP_SCATTERS):
                        pool.wait_ge(scattered[u][g], 16 * n * SWEEP_PAIRS)

            for k in range(PASSES):
                if k == MAX_PASSES:
                    general = flag(pool)
                    with pool.If(general == 0):
                        scatter_adjacency()
                    pool.nop()
                gather_region(k, B)
                if k == 0:
                    gather_search()
                if k < MAX_PASSES:
                    gather_region(k, A)
                    if k == 0:
                        finish_elements()
                    fix_region(k, A)
                else:
                    with pool.If(general == 1):
                        gather_region(k, A)
                        fix_region(k, A)
                    pool.nop()
                fix_region(k, B)
                if k == 0:
                    pool.wait_ge(ends_ready, 1)
                    pool.wait_ge(weights_in, 16 * 5)
                last = ends if k < MAX_PASSES else ends_b
                for t in range(NT):
                    pool.indirect_dma_start(
                        out=agg[:, t * D:(t + 1) * D], out_offset=None, in_=states,
                        in_offset=bass.IndirectOffsetOnAxis(ap=last[:, t:t + 1], axis=0),
                    ).then_inc(agg_in[t // (2 * PER_GROUP)], 16)

        @block.scalar
        def _(sc):
            sc.wait_ge(zeroed, 10)
            for n, (_, b) in enumerate(ROWS_FROM):
                sc.dma_start(bias_f[0:PARTS:32, n * D:(n + 1) * D],
                             b.rearrange("(a f) -> a f", a=1).broadcast_to([len(PART_AT), D])).then_inc(biases_in, 16)
            for n, w in enumerate(W_FROM):
                sc.dma_start(w_all[0:D, n, 0:D], w).then_inc(params_in, 16)
                sc.dma_start(w_all[D:P, n, D:P], w).then_inc(params_in, 16)
            for n, (_, b) in enumerate(COLS_FROM):
                for half in range(2):
                    sc.dma_start(cols[half * D:(half + 1) * D, n:n + 1],
                                 b.rearrange("(f a) -> f a", a=1),
                                 allow_slow_non_contiguous=True).then_inc(params_in, 16)

            def copy_transposed(phase, g, to, free):
                sc.wait_ge(transposed, nth("transposed", phase, g))
                if free is not None:
                    sc.wait_ge(*free)
                n = (GROUPS[g][1] - GROUPS[g][0]) * P
                sc.copy(to[:, 0:n], ps_t[g % 2][:, 0:n]).then_inc(copied, 1)

            sc.wait_ge(ln_centred, 1)
            sc.activation(feat[:, :], node[:, :], ACT.Square).then_inc(ln_squared, 1)
            sc.wait_ge(ln_var, 1)
            sc.activation(stat[:, 3, :], stat[:, 2, :], ACT.Sqrt).then_inc(ln_root, 1)
            for g in range(NG):
                copy_transposed(0, g, feat[:, span(g)], None)
            def convert_search():
                for t in range(NT + 1):
                    s = t % SEARCH_SLOTS
                    sc.wait_ge(row_in[s], 16 * (t // SEARCH_SLOTS + 1))
                    if t >= SEARCH_SLOTS:
                        sc.wait_ge(row_counted, t - SEARCH_SLOTS + 1)
                    sc.copy(search_f[:, s, :], search_i[:, s, :]).then_inc(row_f, 1)

            def stage_half(k, r, half, turn):
                here = slice(half * HALF, (half + 1) * HALF)
                there = bass.ds(turn * TURN + (FIRST_COL[r] + half * HALF), HALF)
                sc.copy(idx_st[:, here], src[:, there]).then_inc(idx_staged[r], 1)
                sc.copy(same_st[:, here], same[:, there]).then_inc(same_staged[r], 1)
                if k >= MAX_PASSES:
                    sc.copy(weight_st[:, here], weight[:, there]).then_inc(weight_staged[r], 1)

            def support_region(k, r):
                for half in range(2):
                    if r == A:
                        sc.wait_ge(step_done[B], (k + 1) * STEPS_B - TURN + (half + 1) * HALF)
                    elif k:
                        sc.wait_ge(step_done[B], k * STEPS_B)
                    stage_half(k, r, half, 0)

                def store_turn(turn, last):
                    for s in range(SLOTS):
                        sc.wait_ge(step_done[r], turn * TURN + (k * REGION_STEPS[r] + (s + 1) * SLOT_STEPS))
                        sc.dma_start(states_rows[r][:, bass.ds(turn * (TURN * D) + s * SLOT_STEPS * D, SLOT_STEPS * D)],
                                     state[:, s, :, :].rearrange("p j f -> p (j f)")).then_inc(stored[r][s], 16)
                        if s % 2 and not last:
                            stage_half(k, r, s // 2, turn + 1)

                with sc.Fori(0, TURNS[r] - 1) as turn:
                    store_turn(turn, False)
                store_turn(TURNS[r] - 1, True)

            def stage_pair(pair, first):
                U16 = mybir.dt.uint16
                elems = scatter_idx.bitcast(U16).rearrange("p (c j h) -> p c j h", j=MAX_DEGREE, h=2)
                to = idx_st[:, :].bitcast(U16).rearrange("p (c h) -> p c h", h=2)
                w = weight[:, 0:STEPS_A].rearrange("p (c j) -> p c j", j=MAX_DEGREE)
                for u in range(2):
                    if not first:
                        for g, n in enumerate(GROUP_SCATTERS):
                            sc.wait_ge(scattered[u][g], pair * (16 * n))
                    here = slice(u * SCATTERS, (u + 1) * SCATTERS)
                    sc.copy(weight_st[:, here, None], w[:, :, bass.ds(pair * 2 + u, 1)]).then_inc(sweep_staged, 1)
                    sc.copy(to[:, here, :], elems[:, :, bass.ds(pair * 2 + u, 1), :].rearrange("p c j h -> p c (j h)")
                            ).then_inc(sweep_staged, 1)

            def stage_sweeps():
                with sc.Fori(1, SWEEP_PAIRS) as pair:
                    stage_pair(pair, False)
                for u in range(2):
                    for g, n in enumerate(GROUP_SCATTERS):
                        sc.wait_ge(scattered[u][g], 16 * n * SWEEP_PAIRS)

            for k in range(PASSES):
                if k == 0:
                    sc.wait_ge(edges_in, 16 * 10)
                    sc.wait_ge(same_ready, 2)
                if k == MAX_PASSES:
                    with sc.If(general == 0):
                        stage_sweeps()
                    sc.nop()
                support_region(k, B)
                if k == 0:
                    convert_search()
                if k < MAX_PASSES:
                    support_region(k, A)
                    if k == MAX_PASSES - 1:
                        sc.wait_ge(weights_in, 16 * 5)
                        sc.wait_ge(elems_ready, 2)
                        general = flag(sc)
                        with sc.If(general == 0):
                            stage_pair(0, True)
                        sc.nop()
                else:
                    with sc.If(general == 1):
                        support_region(k, A)
                        for c in range(CHUNKS):
                            sc.memzero(tiles_of(feat)[:, c * (CHUNK_TILES // 2):(c + 1) * (CHUNK_TILES // 2), :]
                                       ).then_inc(dense_out, 1)
                    with sc.Else():
                        sc.wait_ge(chunk_used, (k - MAX_PASSES + 1) * NT * CHUNKS)
                        for c in range(CHUNKS):
                            sc.copy(tiles_of(feat)[:, c * (CHUNK_TILES // 2):(c + 1) * (CHUNK_TILES // 2), :],
                                    ps_dense[c][:, 0:HALF_CHUNK].rearrange("p (q n) -> p q n", n=DENSE_P)
                                    ).then_inc(dense_out, 1)
                    sc.nop()

                phase = k + 1
                if k < MAX_PASSES:
                    for g in range(NG):
                        uses = "mixed" if k == 0 else "projected"
                        free = None
                        if g >= 2:
                            free = (mixed, nth("mixed", phase, g - 2)) if k == 0 else \
                                (projected, nth("projected", phase, g - 2))
                        copy_transposed(phase, g, agg_t[:, g % 2, :], free)
                        if k == 0:
                            if g == 0:
                                sc.wait_ge(params_in, PARAMS)
                            sc.wait_ge(mixed, nth("mixed", phase, g))
                            n = (GROUPS[g][1] - GROUPS[g][0]) * P
                            sc.activation(feat[:, span(g)], ps_f[g % 2][:, 0:n], ACT.Tanh,
                                          bias=COL["out1"]).then_inc(activated, 1)
                        else:
                            sc.wait_ge(ln_var, g + 2)
                            t0, t1 = 2 * GROUPS[g][0], 2 * GROUPS[g][1]
                            sc.activation(stat[:, 3, t0:t1], stat[:, 2, t0:t1], ACT.Sqrt).then_inc(ln_root, 1)
                else:
                    i = k - MAX_PASSES
                    for g in range(NG):
                        copy_transposed(phase, g, agg_t[:, g % 2, :],
                                        (mixed, nth("mixed", phase, g - 2)) if g >= 2 else None)
                        sc.wait_ge(mixed, nth("mixed", phase, g))
                        n = (GROUPS[g][1] - GROUPS[g][0]) * P
                        sc.activation(feat[:, span(g)], ps_f[g % 2][:, 0:n], ACT.Identity,
                                      bias=COL[f"b1_{i}"]).then_inc(activated, 1)
                    sc.wait_ge(bn_in, 3 * i + 3)
                    sc.activation(bn_std[:, :], bn_var[:, :], ACT.Sqrt).then_inc(bn_root, 1)
                    sc.wait_ge(bn_ready, i + 1)
                    for g in range(NG):
                        sc.activation(feat[:, span(g)], feat[:, span(g)], ACT.Relu, bias=bn_shift[:, :],
                                      scale=bn_scale[:, :]).then_inc(normed, 1)

        @block.vector
        def _(v):
            owned = [0]

            def then(instruction):
                owned[0] += 1
                instruction.then_inc(own, 1)
                v.wait_ge(own, owned[0])

            v.memset(x_res[:, LAST_ROWS * D:], 0.0).then_inc(zeroed, 1)
            v.memset(dst[0:1, 0:1 + PADS], -1).then_inc(zeroed, 1)
            v.memset(src[0:1, 0:PADS], 0).then_inc(zeroed, 1)
            v.memset(weight[0:1, 0:PADS], 0.0).then_inc(zeroed, 1)
            v.memset(zeros[:, :], 0.0).then_inc(zeroed, 1)
            v.memset(carry[:, :, :], 0.0).then_inc(zeroed, 1)
            v.memset(ones[:, :], 1.0).then_inc(zeroed, 1)
            v.memset(w_all[:, :, :], 0.0).then_inc(zeroed, 1)
            v.memset(bias_ones[:, :], 1.0).then_inc(zeroed, 1)
            v.memset(bias_f, 0.0).then_inc(zeroed, 1)
            v.memset(bias_parts[:, :], 0.0).then_inc(zeroed, 1)

            v.wait_ge(x_in, 48)
            then(v.tensor_reduce(stat[:, 0, :], by_tile(x_res[:, :]), AX.X, ALU.add))
            then(v.tensor_scalar(stat[:, 1, :], stat[:, 0, :], -1.0 / D, None, ALU.mult))
            v.tensor_tensor(by_tile(node[:, :]), by_tile(x_res[:, :]),
                            stat[:, 1, :, None].broadcast_to([P, NT, D]), ALU.add).then_inc(ln_centred, 1)
            v.wait_ge(sample_in, 16)
            v.tensor_copy(sample_f, sample_i).then_inc(sample_ready, 1)
            v.wait_ge(ln_squared, 1)
            then(v.tensor_reduce(stat[:, 0, :], by_tile(feat[:, :]), AX.X, ALU.add))
            v.tensor_scalar(stat[:, 2, :], stat[:, 0, :], 1.0 / D, LN_EPS, ALU.mult, ALU.add).then_inc(ln_var, 1)
            v.wait_ge(ln_root, 1)
            then(v.reciprocal(stat[:, 0, :], stat[:, 3, :]))
            v.scalar_tensor_tensor(by_tile(node[:, :]), by_tile(node[:, :]), 0.0,
                                   stat[:, 0, :, None].broadcast_to([P, NT, D]), ALU.max, ALU.mult).then_inc(ln_ready, 1)

            v.wait_ge(biases_in, 16 * len(ROWS_FROM))
            v.wait_ge(zeroed, 11)
            rest = bias_f
            for n, at in enumerate(PART_AT):
                then(v.tensor_copy(bias_split[n], rest))
                if n < len(PART_AT) - 1:
                    then(v.tensor_tensor(bias_rest, rest, bias_split[n], ALU.subtract))
                    rest = bias_rest
                v.tensor_copy(bias_parts[at:at + 1, :], bias_split[n][at:at + 1, :]).then_inc(biases_ready, 1)

            v.wait_ge(edges_in, 16 * 10)
            v.wait_ge(zeroed, 6)
            for r in (A, B):
                n = REGION_STEPS[r]
                v.tensor_tensor(same[:, FIRST_COL[r]:FIRST_COL[r] + n], dst_at[r][:, 1:n + 1], dst_at[r][:, 0:n],
                                ALU.is_equal).then_inc(same_ready, 1)

            def emit_relu(phase, g):
                v.wait_ge(projected, nth("projected", phase, g))
                n = (GROUPS[g][1] - GROUPS[g][0]) * P
                v.tensor_scalar(node[:, span(g)], ps_m[g % 2][:, 0:n], 0.0, None, ALU.max).then_inc(emitted, 1)

            for g in range(NG):
                emit_relu(0, g)

            def start_search():
                for r in (A, B):
                    n = REGION_STEPS[r]
                    then(v.tensor_tensor(lead_flags[:, 0:n], dst_at[r][:, 1:n + 1], dst_at[r][:, 0:1].broadcast_to([P, n]),
                                         ALU.is_equal))
                    then(v.tensor_reduce(lead[:, r:r + 1], lead_flags[:, 0:n], AX.X, ALU.add))
                    v.tensor_scalar(whole[:, r:r + 1], lead[:, r:r + 1], float(n), None, ALU.is_equal).then_inc(lead_ready, 1)
                then(v.tensor_scalar(cont[:, :], lead[:, :], 0.0, None, ALU.is_gt))
                v.wait_ge(consts, 5)
                then(v.tensor_copy(fix_f[:, :], base_i[:, :]))
                then(v.tensor_scalar(lead[:, :], lead[:, :], -1.0, 0.0, ALU.add, ALU.max))
                then(v.tensor_tensor(fix_row[:, :], fix_f[:, :], lead[:, :], ALU.add))
                v.wait_ge(samples_ps, 1)
                for h, bank in enumerate(ps_f):
                    then(v.tensor_copy(samples[:, h * HALF_SAMPLES:(h + 1) * HALF_SAMPLES], bank[:, 0:HALF_SAMPLES]))
                v.wait_ge(whole_ps, 1)
                then(v.tensor_copy(whole_t[:, :, :], ps_tail[0:D, 0:2 * P].rearrange("p (r n) -> p r n", r=2)))
                v.tensor_copy(nval[:, :], nval_i[:, :]).then_inc(tile_counted, 1)

            def count_tiles(turn):
                for c in range(SEARCH_TILES):
                    t = bass.ds(turn * SEARCH_TILES + (c - SEARCH_TILES), 1)
                    v.wait_ge(tile_counted, turn * SEARCH_TILES + (c - SEARCH_TILES + 1))
                    v.tensor_scalar(row_flags, samples[:, :], nval[:, t], None, ALU.is_le, ALU.add,
                                    accum_out=cnt_rows[:, t]).then_inc(tile_counted, 1)

            def ask_rows():
                v.wait_ge(tile_counted, NT + 2)
                then(v.tensor_scalar(cnt_rows[:, :], cnt_rows[:, :], float(E_ROWS - 1), None, ALU.min))
                v.tensor_copy(row_idx[:, :], cnt_rows[:, :]).then_inc(row_wanted, 1)

            def finish_search():
                for t in range(NT + 1):
                    v.wait_ge(row_f, t + 1)
                    v.tensor_scalar(search_flags, search_f[:, t % SEARCH_SLOTS, :],
                                    nval[:, t:t + 1], None, ALU.is_le, ALU.add,
                                    accum_out=cnt_in[:, t:t + 1]).then_inc(row_counted, 1)
                    v.wait_ge(row_counted, t + 1)
                then(v.scalar_tensor_tensor(cnt[:, :], cnt_rows[:, :], float(ROW), cnt_in[:, :], ALU.mult, ALU.add))
                then(v.tensor_tensor(some[:, :], cnt[:, 1:NT + 1], cnt[:, 0:NT], ALU.is_gt))
                then(v.scalar_tensor_tensor(ends_f[:, :], cnt[:, 1:NT + 1], float(PADS - 1 - ZERO_ROW), some[:, :],
                                            ALU.add, ALU.mult))
                then(v.tensor_scalar(ends_f[:, :], ends_f[:, :], float(ZERO_ROW), None, ALU.add))
                then(v.tensor_copy(ends[:, :], ends_f[:, :]))
                then(v.tensor_tensor(in_b[:, :], cnt[:, 1:NT + 1], cnt[:, 0:NT], ALU.subtract))
                then(v.tensor_reduce(guard[:, 0:1], in_b[:, :], AX.X, ALU.max))
                v.tensor_copy(guard[:, 1:2], cnt[:, NT:NT + 1]).then_inc(guard_ready, 1)
                v.wait_ge(guard_ps, 1)
                then(v.tensor_reduce(guard_row[:, 0:1], ps_tail[0:1, 0:P], AX.X, ALU.max))
                then(v.tensor_scalar(guard_row[:, 0:1], guard_row[:, 0:1], float(MAX_DEGREE), None, ALU.is_gt))
                then(v.tensor_scalar(guard_row[:, 1:2], ps_tail[0:1, P + DENSE_P - 1:P + DENSE_P], float(EDGES_A), None,
                                     ALU.is_lt))
                then(v.tensor_tensor(general_f[:, :], guard_row[:, 0:1], guard_row[:, 1:2], ALU.max))
                v.tensor_copy(general_i[:, :], general_f[:, :]).then_inc(flag_ready, 1)
                v.wait_ge(guard_ps, 2)
                then(v.tensor_scalar(dense_f[:, :], ps_bn[:, 0:1], -1.0, 1.0, ALU.mult, ALU.add))
                then(v.tensor_scalar(in_b[:, :], ends_f[:, :], float(FIRST_ROW[B]), dense_f[:, :], ALU.is_lt, ALU.mult))
                then(v.tensor_scalar(some[:, :], ends_f[:, :], -1.0, float(ZERO_ROW), ALU.mult, ALU.add))
                then(v.tensor_tensor(some[:, :], some[:, :], in_b[:, :], ALU.mult))
                v.tensor_tensor(ends_b[:, :], ends_f[:, :], some[:, :], ALU.add).then_inc(ends_ready, 1)

            last_state = state[:, SLOTS - 1, SLOT_STEPS - 1, :]

            def scatter_elements():
                p_part = idx_hi
                off = scatter_idx.bitcast(F32)
                source = src[:, 0:STEPS_A]
                then(v.tensor_scalar(p_part, scatter_idx, 1.0 / NT, 0.5 / NT - 0.5, ALU.mult, ALU.add))
                then(v.scalar_tensor_tensor(t_part, p_part, -float(NT), scatter_idx, ALU.mult, ALU.add))
                then(v.tensor_scalar(off, t_part, 0.0, None, ALU.is_lt))
                then(v.tensor_tensor(p_part, p_part, off, ALU.subtract))
                then(v.scalar_tensor_tensor(t_part, off, float(NT), t_part, ALU.mult, ALU.add))
                then(v.tensor_scalar(off, t_part, float(NT), None, ALU.is_ge))
                then(v.tensor_tensor(p_part, p_part, off, ALU.add))
                then(v.scalar_tensor_tensor(t_part, off, -float(NT), t_part, ALU.mult, ALU.add))
                v.scalar_tensor_tensor(scatter_idx, t_part, float(DENSE_P), p_part, ALU.mult, ALU.add
                                       ).then_inc(cols_ready, 1)
                v.wait_ge(cols_ready, 1)
                then(v.tensor_scalar(idx_hi, source, float(DENSE >> DENSE_SHIFT), None, ALU.mult))
                v.tensor_scalar(idx_hi, idx_hi, DENSE_SHIFT, None, ALU.logical_shift_left).then_inc(cols_ready, 1)

            def fold_region(k, r):
                weighs = k >= MAX_PASSES
                op = ALU.add if weighs else ALU.max
                turns, steps = TURNS[r], REGION_STEPS[r]
                landed = TURNS[B] if r == A else 0

                def fold_turn(turn, first):
                    for s in range(SLOTS):
                        half, at = divmod(s * SLOT_STEPS, HALF)
                        v.wait_ge(gathered[k][s], turn * (16 * SLOT_STEPS) + 16 * SLOT_STEPS * (landed + 1))
                        if at == 0:
                            v.wait_ge(same_staged[r], turn * 2 + (k * 2 * turns + half + 1))
                            if weighs:
                                v.wait_ge(weight_staged[r], turn * 2 + ((k - MAX_PASSES) * 2 * turns + half + 1))
                        if weighs:
                            w = weight_st[:, s * SLOT_STEPS:(s + 1) * SLOT_STEPS]
                            v.tensor_tensor(rows[:, s, :, :], rows[:, s, :, :],
                                            w[:, :, None].broadcast_to([P, SLOT_STEPS, D]), ALU.mult).then_inc(weighted[r], 1)
                            v.wait_ge(weighted[r], turn * SLOTS + ((k - MAX_PASSES) * SLOTS * turns + s + 1))
                        if not first:
                            v.wait_ge(stored[r][s], turn * 16 + 16 * turns * k)
                        elif r == A:
                            v.wait_ge(stored[B][s], 16 * TURNS[B] * (k + 1))
                        for i in range(SLOT_STEPS):
                            j = s * SLOT_STEPS + i
                            before = state[:, s, i - 1, :] if i else state[:, (s - 1) % SLOTS, SLOT_STEPS - 1, :]
                            if first and j == 0:
                                before = zeros[:, 0:D]
                            else:
                                v.wait_ge(step_done[r], turn * TURN + (k * steps + j))
                            v.scalar_tensor_tensor(state[:, s, i, :], before, same_st[:, j:j + 1], rows[:, s, i, :],
                                                   ALU.mult, op).then_inc(step_done[r], 1)

                fold_turn(0, True)
                rest = 1
                if k == 0 and r == B:
                    rest = 1 + SEARCH_TURNS
                    start_search()
                    with v.Fori(1, rest) as turn:
                        fold_turn(turn, False)
                        count_tiles(turn)
                    ask_rows()
                with v.Fori(rest, turns) as turn:
                    fold_turn(turn, False)
                v.wait_ge(step_done[r], (k + 1) * steps)
                v.tensor_copy(finals[:, r, :], last_state).then_inc(final_ready[r], 1)
                v.wait_ge(final_ready[r], k + 1)

            def fix_region(k, r):
                op = ALU.add if k >= MAX_PASSES else ALU.max
                before = 0.0 if r == A else carry[:, A, P:P + 1]
                if r == B:
                    then(v.tensor_copy(carry[:, B, 0:1], carry[:, A, P:P + 1]))
                v.wait_ge(tail_t[r], k + 1)
                v.tensor_tensor_scan(carry[:, r, 1:P + 1], whole_t[:, r, :], ps_tail[0:D, r * P:(r + 1) * P], before,
                                     ALU.mult, op).then_inc(carried[r], 1)
                v.wait_ge(carry_t[r], k + 1)
                v.wait_ge(fix_in[r], 16 * (k + 1))
                v.scalar_tensor_tensor(fixed_rows[:, r, :], ps_carry[r], cont[:, r:r + 1], fixed_rows[:, r, :],
                                       ALU.mult, op).then_inc(fixed[r], 1)
                v.wait_ge(carried[r], k + 1)

            for k in range(PASSES):
                if k == MAX_PASSES:
                    general = flag(v)
                    with v.If(general == 0):
                        v.memset(carry[:, A, P:P + 1], 0.0).then_inc(carry_set, 1)
                    with v.Else():
                        v.memset(bn_dev[:, :], 0.0).then_inc(carry_set, 1)
                    v.wait_ge(carry_set, 1)
                fold_region(k, B)
                if k == 0:
                    finish_search()
                    scatter_elements()
                if k < MAX_PASSES:
                    fold_region(k, A)
                    fix_region(k, A)
                else:
                    with v.If(general == 1):
                        fold_region(k, A)
                        fix_region(k, A)
                    v.nop()
                fix_region(k, B)

                phase = k + 1
                if k == 0:
                    for g in range(NG):
                        emit_relu(phase, g)
                elif k == 1:
                    for g in range(NG):
                        a, b = GROUPS[g]
                        t0, t1, n = 2 * a, 2 * b, (b - a) * P
                        v.wait_ge(projected, nth("projected", phase, g))
                        then(v.tensor_tensor(x_res[:, span(g)], x_res[:, span(g)], ps_m[g % 2][:, 0:n], ALU.add))
                        then(v.tensor_reduce(stat[:, 0, t0:t1], by_tile(x_res[:, span(g)]), AX.X, ALU.add))
                        then(v.tensor_scalar(stat[:, 1, t0:t1], stat[:, 0, t0:t1], -1.0 / D, None, ALU.mult))
                        then(v.tensor_tensor(by_tile(centred[:, 0:n]), by_tile(x_res[:, span(g)]),
                                             stat[:, 1, t0:t1, None].broadcast_to([P, t1 - t0, D]), ALU.add))
                        then(v.tensor_tensor(squares[:, 0:n], centred[:, 0:n], centred[:, 0:n], ALU.mult))
                        then(v.tensor_reduce(stat[:, 0, t0:t1], by_tile(squares[:, 0:n]), AX.X, ALU.add))
                        v.tensor_scalar(stat[:, 2, t0:t1], stat[:, 0, t0:t1], 1.0 / D, LN_EPS,
                                        ALU.mult, ALU.add).then_inc(ln_var, 1)
                        v.wait_ge(ln_root, g + 2)
                        then(v.reciprocal(stat[:, 0, t0:t1], stat[:, 3, t0:t1]))
                        v.scalar_tensor_tensor(by_tile(node[:, span(g)]), by_tile(centred[:, 0:n]), 0.0,
                                               stat[:, 0, t0:t1, None].broadcast_to([P, t1 - t0, D]),
                                               ALU.max, ALU.mult).then_inc(emitted, 1)
                        v.wait_ge(emitted, nth("emitted", phase, g))
                else:
                    i = k - MAX_PASSES

                    def pair_stats(g):
                        v.wait_ge(activated, nth("activated", phase, g))
                        for q in range(*GROUPS[g]):
                            real = P if 2 * q < LAST_ROWS else P - 1
                            last = v.bn_stats(bn[:, q, :], feat[:, q * P:q * P + real])
                        return last

                    def add_dense(g):
                        a, b = GROUPS[g]
                        v.wait_ge(dense_out, CHUNKS * (i + 1))
                        v.wait_ge(copied, nth("copied", phase, g))
                        to = tiles_of(agg_t[:, g % 2, 0:(b - a) * P])
                        v.tensor_tensor(to, to, tiles_of(feat[:, span(g)]), ALU.add).then_inc(dense_added, 1)

                    for g in range(NG):
                        v.wait_ge(agg_in[g], agg_landed(k, g))
                        v.tensor_tensor(agg[:, span(g)], agg[:, span(g)], node[:, span(g)], ALU.add).then_inc(summed, 1)
                        if g >= 1:
                            add_dense(g - 1)
                        if g >= 2:
                            pair_stats(g - 2)
                    add_dense(NG - 1)
                    pair_stats(NG - 2)
                    then(pair_stats(NG - 1))
                    v.bn_aggr(bn_mv[:, :], bn[:, :, :].rearrange("p q s -> p (q s)")).then_inc(bn_in, 1)
                    v.wait_ge(bn_ps, 2 * i + 1)
                    then(v.tensor_copy(bn_mean[:, :], ps_bn[:, 0:1]))
                    then(v.tensor_tensor(bn_dev[:, :], bn_mv[:, 0:1], bn_mean[:, :], ALU.subtract))
                    then(v.tensor_tensor(bn_dev[:, :], bn_dev[:, :], bn_dev[:, :], ALU.mult))
                    v.tensor_tensor(bn_dev[:, :], bn_dev[:, :], bn_mv[:, 1:2], ALU.add).then_inc(bn_in, 1)
                    v.wait_ge(bn_ps, 2 * i + 2)
                    v.tensor_scalar(bn_var[:, :], ps_bn[:, 1:2], BN_EPS, None, ALU.add).then_inc(bn_in, 1)
                    v.wait_ge(bn_root, i + 1)
                    then(v.reciprocal(bn_dev[:, :], bn_std[:, :]))
                    then(v.tensor_tensor(bn_scale[:, :], bn_dev[:, :], COL[f"gamma_{i}"], ALU.mult))
                    then(v.tensor_tensor(bn_mean[:, :], bn_mean[:, :], bn_scale[:, :], ALU.mult))
                    v.tensor_tensor(bn_shift[:, :], COL[f"beta_{i}"], bn_mean[:, :], ALU.subtract).then_inc(bn_ready, 1)
                    for g in range(NG):
                        if k < PASSES - 1:
                            emit_relu(phase, g)
                        else:
                            v.wait_ge(projected, nth("projected", phase, g))
                            n = (GROUPS[g][1] - GROUPS[g][0]) * P
                            v.scalar_tensor_tensor(node[:, span(g)], ps_m[g % 2][:, 0:n], 0.0, x_res[:, span(g)],
                                                   ALU.max, ALU.add).then_inc(emitted, 1)

        @block.tensor
        def _(pe):
            def transpose_group(phase, g, of, ready):
                pe.wait_ge(*ready)
                n = nth("transposed", phase, g)
                if n > 2:
                    pe.wait_ge(copied, n - 2)
                a, b = GROUPS[g]
                for q in range(a, b):
                    last = pe.transpose(ps_t[g % 2][:, (q - a) * P:(q - a + 1) * P], of[:, q * P:(q + 1) * P], ident[:, :])
                last.then_inc(transposed, 1)

            def bank_free(phase, g):
                n = nth("projected", phase, g)
                if n > 2:
                    pe.wait_ge(emitted, n - 2)

            def project(phase, g, bias, parts):
                a, b = GROUPS[g]
                n = (b - a) * P
                pe.matmul(ps_m[g % 2][:, 0:n], bias_ones[:, :], bias.broadcast_to([PARTS, n // D, D]), start=True, stop=False)
                for q in range(a, b):
                    for m, (of, w) in enumerate(parts):
                        last = pe.matmul(ps_m[g % 2][:, (q - a) * P:(q - a + 1) * P],
                                         of[:, (q - a) * P:(q - a + 1) * P], w, start=False,
                                         stop=q == b - 1 and m == len(parts) - 1)
                last.then_inc(projected, 1)

            pe.wait_ge(consts, 9)
            pe.wait_ge(zeroed, 9)
            pe.wait_ge(biases_ready, len(PART_AT))
            pe.wait_ge(params_in, PARAMS)
            for g in range(NG + 1):
                if g < NG:
                    transpose_group(0, g, node, (ln_ready, 1))
                if g >= 1:
                    pe.wait_ge(copied, nth("copied", 0, g - 1))
                    bank_free(0, g - 1)
                    project(0, g - 1, B_ROW["pool1"], [(feat[:, span(g - 1)], W["pool1"])])
            pe.wait_ge(sample_ready, 1)
            for h, bank in enumerate(ps_f):
                last = pe.matmul(bank[:, 0:HALF_SAMPLES], ones[:, :], sample_f[0:1, h * HALF_SAMPLES:(h + 1) * HALF_SAMPLES],
                                 start=True, stop=True)
            last.then_inc(samples_ps, 1)
            pe.wait_ge(lead_ready, 2)
            for r in (A, B):
                last = pe.matmul(ps_tail[0:D, r * P:(r + 1) * P], whole[:, r:r + 1].broadcast_to([P, D]), ident[:, :],
                                 start=True, stop=True)
            last.then_inc(whole_ps, 1)
            pe.wait_ge(guard_ready, 1)
            for n in range(2):
                last = pe.transpose(ps_tail[0:1, n * P:(n + 1) * P], guard[:, n:n + 1], ident[:, :])
            last.then_inc(guard_ps, 1)
            pe.wait_ge(flag_ready, 1)
            pe.matmul(ps_bn[:, 0:1], ones[:, :], general_f[:, :], start=True, stop=True).then_inc(guard_ps, 1)

            def fix_region(k, r):
                pe.wait_ge(final_ready[r], k + 1)
                pe.transpose(ps_tail[0:D, r * P:(r + 1) * P], finals[:, r, :], ident[:, :]).then_inc(tail_t[r], 1)
                pe.wait_ge(carried[r], k + 1)
                pe.transpose(ps_carry[r], carry[:, r, 0:P], ident[0:D, 0:D]).then_inc(carry_t[r], 1)
                pe.wait_ge(fixed[r], k + 1)

            def dense_sums(k):
                i = k - MAX_PASSES

                def source_tiles(turn, first, last):
                    for u in range(DENSE_TILES):
                        pe.wait_ge(x_tile_in[u], turn * 16 + 16 * (i * (NT // DENSE_TILES) + 1))
                        for c in range(CHUNKS):
                            pe.wait_ge(chunk_in[c], turn * (16 * DENSE_TILES) + 16 * (i * NT + u + 1))
                            for h in range(2):
                                mm = pe.matmul(ps_dense[c][h * D:(h + 1) * D, 0:HALF_CHUNK], x_tile[:, u, :],
                                               chunk[:, c, :].rearrange("p (q h m) -> p h q m", h=2, m=DENSE_P)[:, h, :, :],
                                               start=first and u == 0, stop=last and u == DENSE_TILES - 1)
                            mm.then_inc(chunk_used, 1)

                source_tiles(0, True, False)
                with pe.Fori(1, NT // DENSE_TILES - 1) as turn:
                    source_tiles(turn, False, False)
                source_tiles(NT // DENSE_TILES - 1, False, True)

            general = flag(pe)
            for k in range(PASSES):
                if k < MAX_PASSES:
                    fix_region(k, A)
                else:
                    with pe.If(general == 1):
                        fix_region(k, A)
                    with pe.Else():
                        dense_sums(k)
                    pe.nop()
                fix_region(k, B)
                if k >= MAX_PASSES:
                    pe.wait_ge(dense_out, CHUNKS * (k - MAX_PASSES + 1))

                phase = k + 1
                if k == 0:
                    for g in range(NG + 2):
                        if g < NG:
                            transpose_group(phase, g, agg, (agg_in[g], agg_landed(k, g)))
                        if 1 <= g <= NG:
                            c = g - 1
                            n = (GROUPS[c][1] - GROUPS[c][0]) * P
                            pe.wait_ge(copied, nth("copied", phase, c))
                            if c >= 2:
                                pe.wait_ge(activated, nth("activated", phase, c - 2))
                            pe.matmul(ps_f[c % 2][:, 0:n], W["self1"], feat[:, span(c)], start=True, stop=False)
                            pe.matmul(ps_f[c % 2][:, 0:n], W["neigh1"], agg_t[:, c % 2, 0:n], start=False,
                                      stop=True).then_inc(mixed, 1)
                        if g >= 2:
                            c = g - 2
                            pe.wait_ge(activated, nth("activated", phase, c))
                            bank_free(phase, c)
                            project(phase, c, B_ROW["pool2"], [(feat[:, span(c)], W["pool2"])])
                elif k == 1:
                    for g in range(NG + 1):
                        if g < NG:
                            transpose_group(phase, g, agg, (agg_in[g], agg_landed(k, g)))
                        if g >= 1:
                            c = g - 1
                            pe.wait_ge(copied, nth("copied", phase, c))
                            bank_free(phase, c)
                            project(phase, c, B_ROW["out2"],
                                    [(feat[:, span(c)], W["self2"]), (agg_t[:, c % 2, :], W["neigh2"])])
                else:
                    i = k - MAX_PASSES
                    for g in range(NG + 1):
                        if g < NG:
                            transpose_group(phase, g, agg, (summed, nth("summed", phase, g)))
                        if g >= 1:
                            c = g - 1
                            n = (GROUPS[c][1] - GROUPS[c][0]) * P
                            pe.wait_ge(dense_added, nth("summed", phase, c))
                            if nth("mixed", phase, c) > 2:
                                pe.wait_ge(activated, nth("activated", phase, c) - 2)
                            pe.matmul(ps_f[c % 2][:, 0:n], W[f"w1_{i}"], agg_t[:, c % 2, 0:n], start=True,
                                      stop=True).then_inc(mixed, 1)
                    pe.wait_ge(bn_in, 3 * i + 1)
                    pe.matmul(ps_bn[:, 0:1], fold[:, :], bn_mv[:, 0:1], start=True, stop=True).then_inc(bn_ps, 1)
                    pe.wait_ge(bn_in, 3 * i + 2)
                    pe.matmul(ps_bn[:, 1:2], fold[:, :], bn_dev[:, :], start=True, stop=True).then_inc(bn_ps, 1)
                    for g in range(NG):
                        pe.wait_ge(normed, nth("normed", phase, g))
                        bank_free(phase, g)
                        project(phase, g, B_ROW[f"b2_{i}"], [(feat[:, span(g)], W[f"w2_{i}"])])


_INS = ["x", "src", "dst", "edge_weight1",
        "L0_gnn_W_pool1", "L0_gnn_b_pool1", "L0_gnn_W_self1", "L0_gnn_W_neigh1", "L0_gnn_bias1",
        "L0_gnn_W_pool2", "L0_gnn_b_pool2", "L0_gnn_W_self2", "L0_gnn_W_neigh2", "L0_gnn_bias2",
        "L1_gnn_W1", "L1_gnn_b1", "L1_gnn_gamma", "L1_gnn_beta", "L1_gnn_W2", "L1_gnn_b2"]


def kernel(**inputs):
    import concourse.bacc as bacc
    from concourse.bass_utils import run_bass_kernel_spmd

    nc = bacc.Bacc("TRN2", target_bir_lowering=False, num_devices=1)
    arrays, io = {}, {}
    for name in _INS:
        a = np.ascontiguousarray(inputs[name])
        if name == "edge_weight1":
            a = a.reshape(-1)
        arrays[f"in_{name}"] = a
        io[name] = nc.dram_tensor(f"in_{name}", a.shape, mybir.dt.from_np(a.dtype), kind="ExternalInput").ap()
    io["out"] = nc.dram_tensor("out", [N, D], mybir.dt.float32, kind="ExternalOutput").ap()
    build(nc, io)
    r = run_bass_kernel_spmd(nc, [arrays], core_ids=[0])
    return r.results[0]["out"]
```

```python
from contextlib import ExitStack

import numpy as np
import concourse.bass as bass
from concourse import mybir

N, D, E = 12500, 64, 412500
P = 128
NT = -(-N // P)
LAST_ROWS = N - (P - 1) * NT
PAIRS = NT // 2
PER_GROUP = 4
NG = -(-PAIRS // PER_GROUP)
GROUPS = [(PER_GROUP * g, min(PAIRS, PER_GROUP * (g + 1))) for g in range(NG)]

SLOTS, SLOT_STEPS = 4, 13
TURN = SLOTS * SLOT_STEPS
HALF = TURN // 2
A, B = 0, 1
TURNS = (35, 27)
STEPS_A, STEPS_B = (t * TURN for t in TURNS)
REGION_STEPS = (STEPS_A, STEPS_B)
STEPS = STEPS_A + STEPS_B
PADS = P * STEPS - E
EDGES_A = P * STEPS_A - PADS
FIRST_ROW = (0, P * STEPS_A)
FIRST_COL = (0, STEPS_A)
ZERO_ROW = P * STEPS
assert 0 <= PADS < STEPS_A

PART_STEPS = STEPS_A // 2
PART_EDGES = P * PART_STEPS - PADS
DENSE_FROM = (0, 35)
DENSE_TO = (38, 73)
DENSE_P = [b - a for a, b in zip(DENSE_FROM, DENSE_TO)]
DENSE = [n * NT for n in DENSE_P]
DENSE_SHIFT = 2
DENSE_WIDTH = DENSE_TO[-1]
CHUNK_TILES = 14
CHUNK_PAIRS = CHUNK_TILES // 2
CHUNKS = NT // CHUNK_TILES
CHUNK = [CHUNK_TILES * n for n in DENSE_P]
CHUNK_AT = (0, CHUNK[0])
CHUNK_SLOT = sum(CHUNK)
BANK = CHUNK_PAIRS * DENSE_WIDTH
CLEAR = [n // 2 for n in CHUNK]
assert P * NT * max(DENSE) * 4 <= 2 ** 28 and BANK <= 512 and PADS < PART_STEPS
LOW = 71
HIGH = P - LOW
assert 2 * HIGH <= P and LOW <= DENSE_WIDTH
DENSE_TILES = 2
SCATTERS = 13
MAX_DEGREE = PART_STEPS // SCATTERS
SWEEPS = MAX_DEGREE
SCATTER_GROUPS = (0, 4, 7, 10, 13)
PASSES = 5
MAX_PASSES = 2

ROW = 625
E_ROWS = E // ROW
HALF_SAMPLES = E_ROWS // 2
SEARCH_SLOTS = 4
SEARCH_TILES = 9
SEARCH_TURNS = (NT + 1) // SEARCH_TILES
assert SEARCH_TILES * SEARCH_TURNS == NT + 1 and SEARCH_TURNS < TURNS[B]
LN_EPS = BN_EPS = 1e-5


def build(nc, io):
    F32, I32 = mybir.dt.float32, mybir.dt.int32
    ALU, ACT, AX = mybir.AluOpType, mybir.ActivationFunctionType, mybir.AxisListType
    ctx = ExitStack()
    with ctx:
        def sb(name, shape, dt=F32):
            return ctx.enter_context(nc.sbuf_tensor(name, shape, dt))

        def ps(name):
            return ctx.enter_context(nc.psum_tensor(name, [P, 512], F32))

        def sem(name):
            return ctx.enter_context(nc.semaphore(name))

        table = nc.dram_tensor("table", [P * NT, D], F32, kind="Internal").ap()
        states = nc.dram_tensor("states", [P * STEPS + 1, D], F32, kind="Internal").ap()
        table_rows = table.rearrange("(p t) f -> p (t f)", p=P)
        states_rows = [states[FIRST_ROW[r]:FIRST_ROW[r] + P * REGION_STEPS[r], :].rearrange("(p j) f -> p (j f)", p=P)
                       for r in (A, B)]
        adjacency = [nc.dram_tensor(f"adjacency{h}", [P * NT * DENSE[h], 1], F32, kind="Internal").ap() for h in range(2)]
        adjacency_rows = [part.rearrange("(p c) a -> p (c a)", p=P) for part in adjacency]
        dst_rows = io["dst"].rearrange("(r c) -> r c", c=ROW)

        x_res = sb("x_res", [P, NT * D])
        node = sb("node", [P, NT * D])
        agg = sb("agg", [P, NT * D])
        feat_all = sb("feat", [P, max(PAIRS * P, CHUNKS * CHUNK_SLOT)])
        feat = feat_all[:, 0:PAIRS * P]
        chunk = feat_all[:, 0:CHUNKS * CHUNK_SLOT].rearrange("p (c n) -> p c n", n=CHUNK_SLOT)
        x_tile = sb("x_tile", [P, DENSE_TILES, D])
        zeros = sb("zeros", [P, max(BANK, *CLEAR)])
        src = sb("src", [P, STEPS], I32)
        same = sb("same", [P, STEPS])
        weight = sb("weight", [P, STEPS])
        dst = sb("dst_sb", [P, STEPS + 2], I32)
        dst_at = [dst[:, 0:STEPS_A + 1], dst[:, STEPS_A + 1:]]
        scatter_idx = dst[:, 1:STEPS_A + 1]
        scatter_src = node[:, 0:STEPS_A].bitcast(I32)
        idx_st = sb("idx_st", [P, TURN], I32)
        same_st = sb("same_st", [P, TURN])
        weight_st = sb("weight_st", [P, TURN])
        rows = sb("rows", [P, SLOTS, SLOT_STEPS, D])
        state = sb("state", [P, SLOTS, SLOT_STEPS, D])
        samples = agg[:, 0:E_ROWS]
        sample_i = agg[0:1, NT * D - E_ROWS:].bitcast(I32)
        sample_f = agg[0:1, NT * D - 2 * E_ROWS:NT * D - E_ROWS]
        nval_i = sb("nval_i", [P, NT + 1], I32)
        nval = sb("nval", [P, NT + 1])
        cnt_rows = sb("cnt_rows", [P, NT + 1])
        row_idx = sb("row_idx", [P, NT + 1], I32)
        cnt_in = sb("cnt_in", [P, NT + 1])
        cnt = sb("cnt", [P, NT + 1])
        some = sb("some", [P, NT])
        ends_f = sb("ends_f", [P, NT])
        ends = sb("ends", [P, NT], I32)
        ends_low = sb("ends_low", [P, NT], I32)
        ends_b = sb("ends_b", [P, 2, PAIRS], I32)
        ends_high = sb("ends_high", [2 * HIGH, PAIRS], I32)
        low_mask = sb("low_mask", [P, 1])
        in_b = sb("in_b", [P, NT])
        guard = sb("guard", [P, 2])
        guard_row = sb("guard_row", [1, 2 * P])
        dense_f = sb("dense_f", [P, 1])
        general_f = sb("general_f", [1, 1])
        general_i = sb("general_i", [1, 1], I32)
        lead_flags = agg[:, 0:max(REGION_STEPS)]
        lead = sb("lead", [P, 2])
        cont = sb("cont", [P, 2])
        whole = sb("whole", [P, 2])
        fix_f = sb("fix_f", [P, 2])
        base_i = sb("base_i", [P, 2], I32)
        fix_row = sb("fix_row", [P, 2], I32)
        whole_t = sb("whole_t", [D, 2, P])
        carry = sb("carry", [D, 2, P + 1])
        finals = sb("finals", [P, 2, D])
        fixed_rows = sb("fixed_rows", [P, 2, D])
        search_i = agg[:, 0:SEARCH_SLOTS * ROW].bitcast(I32).rearrange("p (s c) -> p s c", c=ROW)
        search_f = agg[:, SEARCH_SLOTS * ROW:2 * SEARCH_SLOTS * ROW].rearrange("p (s c) -> p s c", c=ROW)
        row_flags = agg[:, E_ROWS:2 * E_ROWS]
        search_flags = agg[:, 2 * SEARCH_SLOTS * ROW:(2 * SEARCH_SLOTS + 1) * ROW]
        idx_hi = agg[:, 0:STEPS_A].bitcast(I32)
        t_part = agg[:, STEPS_A:2 * STEPS_A]
        agg_t = sb("agg_t", [P, 2, 512])
        ident = sb("ident", [P, P])
        ones = sb("ones", [1, P])
        stat = sb("stat", [P, 4, NT])
        layer_norm = state[:, :, :, :].rearrange("p s j f -> p (s j f)")
        centred = layer_norm[:, 0:512]
        squares = layer_norm[:, 512:1024]
        bn = sb("bn", [P, PAIRS, 6])
        bn_mv = sb("bn_mv", [P, 2])
        bn_mean = sb("bn_mean", [P, 1])
        bn_dev = sb("bn_dev", [P, 1])
        bn_var = sb("bn_var", [P, 1])
        bn_std = sb("bn_std", [P, 1])
        bn_scale = sb("bn_scale", [P, 1])
        bn_shift = sb("bn_shift", [P, 1])
        fold = sb("fold", [P, P])
        W_NAMES = ["pool1", "self1", "neigh1", "pool2", "self2", "neigh2"] + \
            [f"w1_{i}" for i in range(3)] + [f"w2_{i}" for i in range(3)]
        W_FROM = [io["L0_gnn_W_pool1"], io["L0_gnn_W_self1"], io["L0_gnn_W_neigh1"],
                  io["L0_gnn_W_pool2"], io["L0_gnn_W_self2"], io["L0_gnn_W_neigh2"]] + \
            [io["L1_gnn_W1"][i] for i in range(3)] + [io["L1_gnn_W2"][i] for i in range(3)]
        w_all = sb("w_all", [P, len(W_NAMES), P])
        W = {n: w_all[:, i, :] for i, n in enumerate(W_NAMES)}
        ROWS_FROM = [("pool1", io["L0_gnn_b_pool1"]), ("pool2", io["L0_gnn_b_pool2"]),
                     ("out2", io["L0_gnn_bias2"])] + [(f"b2_{i}", io["L1_gnn_b2"][i]) for i in range(3)]
        BF16 = mybir.dt.bfloat16
        PART_AT = (0, 32, 64)
        PARTS = PART_AT[-1] + 1
        BIASES = len(ROWS_FROM) * D
        bias_parts = sb("bias_parts", [PARTS, BIASES], BF16)
        B_ROW = {n: bias_parts[:, None, i * D:(i + 1) * D] for i, (n, _) in enumerate(ROWS_FROM)}
        bias_ones = sb("bias_ones", [PARTS, P], BF16)
        set_up = state[0:PARTS, :, :, :].rearrange("p s j f -> p (s j f)")
        bias_f, bias_rest = set_up[:, 0:BIASES], set_up[:, BIASES:2 * BIASES]
        bias_split = [set_up[:, 2 * BIASES + n * (BIASES // 2):2 * BIASES + (n + 1) * (BIASES // 2)].bitcast(BF16)
                      for n in range(len(PART_AT))]
        COLS_FROM = [("out1", io["L0_gnn_bias1"])] + [(f"{a}_{i}", io[b][i]) for i in range(3) for a, b in
                     (("b1", "L1_gnn_b1"), ("gamma", "L1_gnn_gamma"), ("beta", "L1_gnn_beta"))]
        cols = sb("cols", [P, len(COLS_FROM)])
        COL = {n: cols[:, i:i + 1] for i, (n, _) in enumerate(COLS_FROM)}

        PARAMS = 16 * (2 * len(W_FROM) + 2 * len(COLS_FROM))

        ps_t = [ps("ps_t0"), ps("ps_t1")]
        ps_f = [ps("ps_f0"), ps("ps_f1")]
        ps_m = [ps("ps_m0"), ps("ps_m1")]
        ps_tail = ps("ps_tail")
        ps_carry = [ps_tail[:, 2 * P + r * D:2 * P + (r + 1) * D] for r in (A, B)]
        ps_bn = ps_tail[:, 2 * P + 2 * D:2 * P + 2 * D + 2]
        ps_dense = [*ps_t, *ps_f, *ps_m, ps("ps_dense6")]

        zeroed = sem("zeroed")
        x_in = sem("x_in")
        edges_in = sem("edges_in")
        weights_in = sem("weights_in")
        weights_a_in = sem("weights_a_in")
        parts_in = sem("parts_in")
        params_in = sem("params_in")
        biases_in = sem("biases_in")
        biases_ready = sem("biases_ready")
        consts = sem("consts")
        sample_in = sem("sample_in")
        sample_ready = sem("sample_ready")
        own = sem("own")
        same_ready = sem("same_ready")
        lead_ready = sem("lead_ready")
        guard_ready = sem("guard_ready")
        guard_ps = sem("guard_ps")
        flag_ready = sem("flag_ready")
        ln_centred = sem("ln_centred")
        ln_squared = sem("ln_squared")
        ln_var = sem("ln_var")
        ln_root = sem("ln_root")
        ln_ready = sem("ln_ready")
        samples_ps = sem("samples_ps")
        tile_counted = sem("tile_counted")
        whole_ps = sem("whole_ps")
        row_wanted = sem("row_wanted")
        row_in = [sem(f"row_in{s}") for s in range(SEARCH_SLOTS)]
        row_f = sem("row_f")
        row_counted = sem("row_counted")
        ends_ready = sem("ends_ready")
        table_in = sem("table_in")
        idx_staged = [sem(f"idx_staged{r}") for r in "AB"]
        same_staged = [sem(f"same_staged{r}") for r in "AB"]
        weight_staged = [sem(f"weight_staged{r}") for r in "AB"]
        gathered = [[sem(f"gathered{k}_{s}") for s in range(SLOTS)] for k in range(PASSES)]
        weighted = [sem(f"weighted{r}") for r in "AB"]
        step_done = [sem(f"step_done{r}") for r in "AB"]
        stored = [[sem(f"stored{r}{s}") for s in range(SLOTS)] for r in "AB"]
        final_ready = [sem(f"final_ready{r}") for r in "AB"]
        tail_t = [sem(f"tail_t{r}") for r in "AB"]
        carry_set = sem("carry_set")
        carried = [sem(f"carried{r}") for r in "AB"]
        carry_t = [sem(f"carry_t{r}") for r in "AB"]
        fix_in = [sem(f"fix_in{r}") for r in "AB"]
        fixed = [sem(f"fixed{r}") for r in "AB"]
        fix_out = [sem(f"fix_out{r}") for r in "AB"]
        cleared = sem("cleared")
        cols_ready = sem("cols_ready")
        elems_ready = sem("elems_ready")
        sweep_staged = sem("sweep_staged")
        scattered = [[sem(f"scattered{u}_{g}") for g in range(4)] for u in range(2)]
        x_tile_in = [sem(f"x_tile_in{u}") for u in range(DENSE_TILES)]
        chunk_in = [sem(f"chunk_in{c}") for c in range(CHUNKS)]
        chunk_used = sem("chunk_used")
        dense_summed = sem("dense_summed")
        dense_out = sem("dense_out")
        dense_added = sem("dense_added")
        low_in = sem("low_in")
        high_in = sem("high_in")
        agg_in = [sem(f"agg_in{g}") for g in range(NG)]
        transposed = sem("transposed")
        copied = sem("copied")
        mixed = sem("mixed")
        activated = sem("activated")
        bn_in = sem("bn_in")
        bn_ps = sem("bn_ps")
        bn_root = sem("bn_root")
        bn_ready = sem("bn_ready")
        normed = sem("normed")
        projected = sem("projected")
        emitted = sem("emitted")
        out_in = sem("out_in")
        IN_PHASES = {"dense_added": (3, 4, 5), "transposed": range(6), "copied": range(6),
                     "mixed": (1, 3, 4, 5), "activated": (1, 3, 4, 5), "normed": (3, 4, 5),
                     "projected": range(6), "emitted": range(6)}

        def nth(event, phase, g):
            return NG * list(IN_PHASES[event]).index(phase) + g + 1

        def agg_landed(k, g):
            pairs = GROUPS[g][1] - GROUPS[g][0]
            return 16 * pairs * (2 * (k + 1) if k < MAX_PASSES else MAX_PASSES + k + 1)

        def span(g):
            a, b = GROUPS[g]
            return slice(a * P, b * P)

        def by_tile(ap):
            return ap.rearrange("p (t f) -> p t f", f=D)

        def flag(engine):
            engine.wait_ge(flag_ready, 1)
            return engine.value_load(general_i[0:1, 0:1], min_val=0, max_val=1)

        def tiles_of(ap):
            return ap.rearrange("p (q n) -> p q n", n=P)[:, :, 0:DENSE_WIDTH]

        GROUP_SCATTERS = [b - a for a, b in zip(SCATTER_GROUPS, SCATTER_GROUPS[1:])]

        block = ctx.enter_context(nc.Block())
        TABLE_DMAS = NG

        @block.sync
        def _(sp):
            x_rows = io["x"][0:(P - 1) * NT, :].rearrange("(p t) f -> p (t f)", t=NT)
            sp.wait_ge(zeroed, 1)
            sp.dma_start(x_res[0:112, :], x_rows[0:112, :]).then_inc(x_in, 16)
            sp.dma_start(x_res[112:P - 1, :], x_rows[112:P - 1, :]).then_inc(x_in, 16)
            sp.dma_start(x_res[P - 1:P, 0:LAST_ROWS * D],
                         io["x"][(P - 1) * NT:N, :].rearrange("(p t) f -> p (t f)", p=1)).then_inc(x_in, 16)
            sp.dma_start(sample_i, io["dst"].rearrange("(r c) -> c r", c=ROW)[ROW - 1:ROW, :],
                         allow_slow_non_contiguous=True).then_inc(sample_in, 16)
            sp.wait_ge(zeroed, 4)
            FIRST = STEPS_A - PADS

            def load_padded(to, name, steps, done):
                first = steps - PADS
                rest = io[name][first:first + (P - 1) * steps].rearrange("(p j) -> p j", j=steps)
                sp.dma_start(to[0:1, PADS:steps], io[name][0:first].rearrange("(p j) -> p j", p=1)).then_inc(done, 16)
                sp.dma_start(to[1:113, :], rest[0:112, :]).then_inc(done, 16)
                sp.dma_start(to[113:P, :], rest[112:P - 1, :]).then_inc(done, 16)

            def load_from(to, name, first, steps, done):
                sp.dma_start(to, io[name][first:first + P * steps].rearrange("(p j) -> p j", j=steps)).then_inc(done, 16)

            def load_parts(to, name, done):
                load_padded(to[:, 0:PART_STEPS], name, PART_STEPS, done)
                load_from(to[:, PART_STEPS:], name, PART_EDGES, PART_STEPS, done)

            load_padded(dst_at[A][:, 1:], "dst", STEPS_A, edges_in)
            load_from(dst_at[B][:, 1:], "dst", EDGES_A, STEPS_B, edges_in)
            for to, first, steps in ((dst_at[A][1:P, 0:1], FIRST - 1, STEPS_A), (dst_at[B][:, 0:1], EDGES_A - 1, STEPS_B)):
                n = to.shape[0]
                sp.dma_start(to, io["dst"][first:first + (n - 1) * steps + 1:steps].rearrange("(p a) -> p a", a=1),
                             allow_slow_non_contiguous=True).then_inc(edges_in, 16)
            load_padded(src[:, 0:STEPS_A], "src", STEPS_A, edges_in)
            load_from(src[:, STEPS_A:], "src", EDGES_A, STEPS_B, edges_in)
            load_from(weight[:, STEPS_A:], "edge_weight1", EDGES_A, STEPS_B, weights_in)
            sp.wait_ge(zeroed, 5)
            sp.dma_start(states[ZERO_ROW:ZERO_ROW + 1, :], zeros[0:1, 0:D]).then_inc(weights_in, 16)

            def store_table(phase):
                for g in range(NG):
                    sp.wait_ge(emitted, nth("emitted", phase, g))
                    sp.dma_start(table_rows[:, span(g)], node[:, span(g)]).then_inc(table_in, 16)

            def clear_tiles(pass_turn, tile):
                at = [[sp.snap(tile * DENSE[h] + u * DENSE[h]) for h in range(2)] for u in range(2)]
                sp.wait_ge(step_done[B], pass_turn * TURN + TURN)
                for u in range(2):
                    for h in range(2):
                        sp.dma_start(adjacency_rows[h][:, bass.ds(at[u][h], DENSE[h])].rearrange("p (c n) -> p c n", n=CLEAR[h]),
                                     zeros[:, None, 0:CLEAR[h]].broadcast_to([P, DENSE[h] // CLEAR[h], CLEAR[h]])
                                     ).then_inc(cleared, 16)

            for k in range(PASSES):
                store_table(k)
                if k == 0:
                    sp.wait_ge(same_ready, 2)
                    sp.wait_ge(lead_ready, 3)
                    load_parts(scatter_idx, "dst", parts_in)
                    load_parts(scatter_src, "src", parts_in)
                    with sp.Fori(0, NT // 4) as i:
                        clear_tiles(i, i * 2)
                    general = flag(sp)
                    with sp.If(general == 0):
                        load_parts(weight[:, 0:STEPS_A], "edge_weight1", weights_a_in)
                    with sp.Else():
                        load_padded(weight[:, 0:STEPS_A], "edge_weight1", STEPS_A, weights_a_in)
                    sp.wait_ge(ends_ready, 1)
                    for h in range(2):
                        sp.dma_start(ends_high[h * HIGH:(h + 1) * HIGH, :], ends_b[LOW:P, h, :]).then_inc(high_in, 16)
                elif k == 1:
                    with sp.Fori(0, NT // 2 - NT // 4) as i:
                        clear_tiles(i + TURNS[B], i * 2 + 2 * (NT // 4))
                else:
                    with sp.If(general == 0):
                        base = (k - MAX_PASSES) * NT
                        sp.wait_ge(table_in, 16 * TABLE_DMAS * (k + 1))
                        if k == MAX_PASSES:
                            for u in range(2):
                                for g, n in enumerate(GROUP_SCATTERS):
                                    sp.wait_ge(scattered[u][g], 16 * n * SWEEPS)

                        def stream(turn, first):
                            for u in range(DENSE_TILES):
                                rows_at = sp.snap(turn * (DENSE_TILES * D) + u * D)
                                for c in range(CHUNKS):
                                    at = [sp.snap(turn * (DENSE_TILES * DENSE[h]) + (u * DENSE[h] + c * CHUNK[h]))
                                          for h in range(2)]
                                    if not (first and u == 0):
                                        sp.wait_ge(chunk_used, turn * (DENSE_TILES * CHUNKS) +
                                                   (base * CHUNKS + (u - 1) * CHUNKS + c + 1))
                                    if c == 0:
                                        sp.dma_start(x_tile[:, u, :], table_rows[:, bass.ds(rows_at, D)]
                                                     ).then_inc(x_tile_in[u], 16)
                                    for h in range(2):
                                        sp.dma_start(chunk[:, c, CHUNK_AT[h]:CHUNK_AT[h] + CHUNK[h]],
                                                     adjacency_rows[h][:, bass.ds(at[h], CHUNK[h])]).then_inc(chunk_in[c], 16)

                        stream(0, True)
                        with sp.Fori(1, NT // DENSE_TILES) as turn:
                            stream(turn, False)
                    sp.nop()

            out_rows = io["out"][0:(P - 1) * NT, :].rearrange("(p t) f -> p (t f)", t=NT)
            for g in range(NG):
                sp.wait_ge(emitted, nth("emitted", PASSES, g))
                sp.dma_start(out_rows[0:112, span(g)], node[0:112, span(g)]).then_inc(out_in, 16)
                sp.dma_start(out_rows[112:P - 1, span(g)], node[112:P - 1, span(g)]).then_inc(out_in, 16)
            sp.dma_start(io["out"][(P - 1) * NT:N, :].rearrange("(p t) f -> p (t f)", p=1),
                         node[P - 1:P, 0:LAST_ROWS * D]).then_inc(out_in, 16)
            sp.wait_ge(out_in, 16 * (2 * NG + 1))

        @block.gpsimd
        def _(pool):
            pool.memset(ident[:, :], 0.0).then_inc(consts, 1)
            pool.memset(fold[:, :], 0.0).then_inc(consts, 1)
            pool.iota(nval_i[:, :], pattern=[[1, NT + 1]], base=-1, channel_multiplier=NT).then_inc(consts, 1)
            pool.iota(base_i[:, 0:1], pattern=[[0, 1]], base=FIRST_ROW[A], channel_multiplier=STEPS_A).then_inc(consts, 1)
            pool.iota(base_i[:, 1:2], pattern=[[0, 1]], base=FIRST_ROW[B], channel_multiplier=STEPS_B).then_inc(consts, 1)
            pool.wait_ge(consts, 5)
            pool.affine_select(out=ident[:, :], in_=ident[:, :], compare_op=ALU.not_equal, fill=1.0,
                               base=0, pattern=[[-1, P]], channel_multiplier=1).then_inc(consts, 1)
            for n, off in enumerate((0, D, -D)):
                pool.affine_select(out=fold[:, :], in_=fold[:, :], compare_op=ALU.not_equal, fill=0.5,
                                   base=off, pattern=[[-1, P]], channel_multiplier=1).then_inc(consts, 1)
                pool.wait_ge(consts, 7 + n)

            staged_next = ctx.enter_context(pool.register("staged_next"))
            scattered_next = [[ctx.enter_context(pool.register(f"scattered_next{u}_{g}")) for g in range(4)]
                              for u in range(2)]

            def gather_search():
                pool.wait_ge(row_wanted, 1)
                for t in range(NT + 1):
                    s = t % SEARCH_SLOTS
                    if t >= SEARCH_SLOTS:
                        pool.wait_ge(row_f, t - SEARCH_SLOTS + 1)
                    pool.indirect_dma_start(
                        out=search_i[:, s, :], out_offset=None, in_=dst_rows,
                        in_offset=bass.IndirectOffsetOnAxis(ap=row_idx[:, t:t + 1], axis=0)).then_inc(row_in[s], 16)

            def gather_region(k, r):
                pool.reg_mov(staged_next, k * 2 * TURNS[r] + 1)

                def gather_turn():
                    for half in range(2):
                        pool.wait_ge(idx_staged[r], staged_next)
                        pool.reg_add(staged_next, staged_next, 1)
                        pool.wait_ge(table_in, 16 * TABLE_DMAS * (k + 1))
                        for j in range(half * HALF, (half + 1) * HALF):
                            s, i = divmod(j, SLOT_STEPS)
                            pool.indirect_dma_start(
                                out=rows[:, s, i, :], out_offset=None, in_=table,
                                in_offset=bass.IndirectOffsetOnAxis(ap=idx_st[:, j:j + 1], axis=0),
                            ).then_inc(gathered[k][s], 16)

                with pool.Fori(0, TURNS[r]) as turn:
                    gather_turn()

            def fix_region(k, r):
                for s in range(SLOTS):
                    pool.wait_ge(stored[r][s], 16 * TURNS[r] * (k + 1))
                fix_at = bass.IndirectOffsetOnAxis(ap=fix_row[:, r:r + 1], axis=0)
                pool.indirect_dma_start(out=fixed_rows[:, r, :], out_offset=None, in_=states,
                                        in_offset=fix_at).then_inc(fix_in[r], 16)
                pool.wait_ge(fixed[r], k + 1)
                pool.indirect_dma_start(out=states, out_offset=fix_at, in_=fixed_rows[:, r, :],
                                        in_offset=None).then_inc(fix_out[r], 16)
                pool.wait_ge(fix_out[r], 16 * (k + 1))

            def finish_elements():
                pool.wait_ge(cols_ready, 1)
                pool.tensor_tensor(scatter_idx, idx_hi, scatter_idx, ALU.add).then_inc(elems_ready, 1)
                pool.wait_ge(elems_ready, 1)
                pool.iota(scatter_idx[0:1, 0:PADS], pattern=[[1, PADS]], base=N * DENSE[0],
                          channel_multiplier=0).then_inc(elems_ready, 1)

            def scatter_adjacency():
                pool.wait_ge(cleared, 16 * 2 * NT)
                pool.reg_mov(staged_next, 2)
                for row in scattered_next:
                    for g, register in enumerate(row):
                        pool.reg_mov(register, 16 * GROUP_SCATTERS[g])

                def wait_landed(h, g):
                    pool.wait_ge(scattered[h][g], scattered_next[h][g])
                    pool.reg_add(scattered_next[h][g], scattered_next[h][g], 16 * GROUP_SCATTERS[g])

                def sweep_parts(first):
                    for h in range(2):
                        pool.wait_ge(sweep_staged, staged_next)
                        pool.reg_add(staged_next, staged_next, 2)
                        for g, n in enumerate(GROUP_SCATTERS):
                            if g == 3:
                                wait_landed(h, 0)
                            elif not first:
                                wait_landed(h, g + 1)
                            for c in range(SCATTER_GROUPS[g], SCATTER_GROUPS[g + 1]):
                                at = h * SCATTERS + c
                                pool.indirect_dma_start(
                                    out=adjacency[h], in_=weight_st[:, at:at + 1], in_offset=None, compute_op=ALU.add,
                                    out_offset=bass.IndirectOffsetOnAxis(ap=idx_st[:, at:at + 1], axis=0),
                                ).then_inc(scattered[h][g], 16)

                sweep_parts(True)
                with pool.Fori(1, SWEEPS) as sweep:
                    sweep_parts(False)
                for h in range(2):
                    for g, n in enumerate(GROUP_SCATTERS):
                        pool.wait_ge(scattered[h][g], 16 * n * SWEEPS)

            for k in range(PASSES):
                if k == MAX_PASSES:
                    general = flag(pool)
                    with pool.If(general == 0):
                        scatter_adjacency()
                    pool.nop()
                gather_region(k, B)
                if k == 0:
                    gather_search()
                if k < MAX_PASSES:
                    gather_region(k, A)
                    if k == 0:
                        finish_elements()
                    fix_region(k, A)
                else:
                    with pool.If(general == 1):
                        gather_region(k, A)
                        fix_region(k, A)
                    pool.nop()
                fix_region(k, B)
                if k == 0:
                    pool.wait_ge(ends_ready, 1)
                    pool.wait_ge(weights_in, 16 * 2)
                if k < MAX_PASSES:
                    for t in range(NT):
                        pool.indirect_dma_start(
                            out=agg[:, t * D:(t + 1) * D], out_offset=None, in_=states,
                            in_offset=bass.IndirectOffsetOnAxis(ap=ends[:, t:t + 1], axis=0),
                        ).then_inc(agg_in[t // (2 * PER_GROUP)], 16)
                else:
                    with pool.If(general == 1):
                        for t in range(NT):
                            pool.indirect_dma_start(
                                out=agg[:, t * D:(t + 1) * D], out_offset=None, in_=states,
                                in_offset=bass.IndirectOffsetOnAxis(ap=ends_low[:, t:t + 1], axis=0),
                            ).then_inc(low_in, 16)
                        pool.wait_ge(dense_summed, k - MAX_PASSES + 1)
                    pool.nop()
                    pool.wait_ge(high_in, 16 * 2)
                    for q in range(PAIRS):
                        pool.indirect_dma_start(
                            out=agg[0:2 * HIGH, q * D:(q + 1) * D], out_offset=None, in_=states,
                            in_offset=bass.IndirectOffsetOnAxis(ap=ends_high[:, q:q + 1], axis=0),
                        ).then_inc(agg_in[q // PER_GROUP], 16)

        @block.scalar
        def _(sc):
            sc.wait_ge(zeroed, 10)
            for n, (_, b) in enumerate(ROWS_FROM):
                sc.dma_start(bias_f[0:PARTS:32, n * D:(n + 1) * D],
                             b.rearrange("(a f) -> a f", a=1).broadcast_to([len(PART_AT), D])).then_inc(biases_in, 16)
            for n, w in enumerate(W_FROM):
                sc.dma_start(w_all[0:D, n, 0:D], w).then_inc(params_in, 16)
                sc.dma_start(w_all[D:P, n, D:P], w).then_inc(params_in, 16)
            for n, (_, b) in enumerate(COLS_FROM):
                for half in range(2):
                    sc.dma_start(cols[half * D:(half + 1) * D, n:n + 1],
                                 b.rearrange("(f a) -> f a", a=1),
                                 allow_slow_non_contiguous=True).then_inc(params_in, 16)

            def copy_transposed(phase, g, to, free):
                sc.wait_ge(transposed, nth("transposed", phase, g))
                if free is not None:
                    sc.wait_ge(*free)
                n = (GROUPS[g][1] - GROUPS[g][0]) * P
                sc.copy(to[:, 0:n], ps_t[g % 2][:, 0:n]).then_inc(copied, 1)

            sc.wait_ge(ln_centred, 1)
            sc.activation(feat[:, :], node[:, :], ACT.Square).then_inc(ln_squared, 1)
            sc.wait_ge(ln_var, 1)
            sc.activation(stat[:, 3, :], stat[:, 2, :], ACT.Sqrt).then_inc(ln_root, 1)
            for g in range(NG):
                copy_transposed(0, g, feat[:, span(g)], None)
            def convert_search():
                for t in range(NT + 1):
                    s = t % SEARCH_SLOTS
                    sc.wait_ge(row_in[s], 16 * (t // SEARCH_SLOTS + 1))
                    if t >= SEARCH_SLOTS:
                        sc.wait_ge(row_counted, t - SEARCH_SLOTS + 1)
                    sc.copy(search_f[:, s, :], search_i[:, s, :]).then_inc(row_f, 1)

            def stage_half(k, r, half, turn):
                here = slice(half * HALF, (half + 1) * HALF)
                there = bass.ds(turn * TURN + (FIRST_COL[r] + half * HALF), HALF)
                sc.copy(idx_st[:, here], src[:, there]).then_inc(idx_staged[r], 1)
                sc.copy(same_st[:, here], same[:, there]).then_inc(same_staged[r], 1)
                if k >= MAX_PASSES:
                    sc.copy(weight_st[:, here], weight[:, there]).then_inc(weight_staged[r], 1)

            def support_region(k, r):
                for half in range(2):
                    if r == A:
                        sc.wait_ge(step_done[B], (k + 1) * STEPS_B - TURN + (half + 1) * HALF)
                    elif k:
                        sc.wait_ge(step_done[B], k * STEPS_B)
                    stage_half(k, r, half, 0)

                def store_turn(turn, last):
                    for s in range(SLOTS):
                        sc.wait_ge(step_done[r], turn * TURN + (k * REGION_STEPS[r] + (s + 1) * SLOT_STEPS))
                        sc.dma_start(states_rows[r][:, bass.ds(turn * (TURN * D) + s * SLOT_STEPS * D, SLOT_STEPS * D)],
                                     state[:, s, :, :].rearrange("p j f -> p (j f)")).then_inc(stored[r][s], 16)
                        if s % 2 and not last:
                            stage_half(k, r, s // 2, turn + 1)

                with sc.Fori(0, TURNS[r] - 1) as turn:
                    store_turn(turn, False)
                store_turn(TURNS[r] - 1, True)

            def stage_sweep(sweep, first):
                U16 = mybir.dt.uint16
                to = idx_st[:, :].bitcast(U16).rearrange("p (c h) -> p c h", h=2)
                for h in range(2):
                    part = slice(h * PART_STEPS, (h + 1) * PART_STEPS)
                    elems = scatter_idx[:, part].bitcast(U16).rearrange("p (c j h) -> p c j h", j=MAX_DEGREE, h=2)
                    w = weight[:, part].rearrange("p (c j) -> p c j", j=MAX_DEGREE)
                    if not first:
                        for g, n in enumerate(GROUP_SCATTERS):
                            sc.wait_ge(scattered[h][g], sweep * (16 * n))
                    here = slice(h * SCATTERS, (h + 1) * SCATTERS)
                    sc.copy(weight_st[:, here, None], w[:, :, bass.ds(sweep, 1)]).then_inc(sweep_staged, 1)
                    sc.copy(to[:, here, :], elems[:, :, bass.ds(sweep, 1), :].rearrange("p c j h -> p c (j h)")
                            ).then_inc(sweep_staged, 1)

            def stage_sweeps():
                with sc.Fori(1, SWEEPS) as sweep:
                    stage_sweep(sweep, False)
                for h in range(2):
                    for g, n in enumerate(GROUP_SCATTERS):
                        sc.wait_ge(scattered[h][g], 16 * n * SWEEPS)

            for k in range(PASSES):
                if k == 0:
                    sc.wait_ge(edges_in, 16 * 10)
                    sc.wait_ge(same_ready, 2)
                if k == MAX_PASSES:
                    with sc.If(general == 0):
                        stage_sweeps()
                    sc.nop()
                support_region(k, B)
                if k == 0:
                    convert_search()
                if k < MAX_PASSES:
                    support_region(k, A)
                    if k == MAX_PASSES - 1:
                        sc.wait_ge(weights_in, 16 * 2)
                        sc.wait_ge(elems_ready, 2)
                        general = flag(sc)
                        with sc.If(general == 0):
                            sc.wait_ge(weights_a_in, 16 * 4)
                            stage_sweep(0, True)
                        sc.nop()
                else:
                    with sc.If(general == 1):
                        sc.wait_ge(weights_a_in, 16 * 3)
                        support_region(k, A)
                    sc.nop()
                    sc.wait_ge(dense_summed, k - MAX_PASSES + 1)
                    for c in range(CHUNKS):
                        sc.copy(tiles_of(feat)[:, c * CHUNK_PAIRS:(c + 1) * CHUNK_PAIRS, :],
                                ps_dense[c][:, 0:BANK].rearrange("p (q n) -> p q n", n=DENSE_WIDTH)
                                ).then_inc(dense_out, 1)

                phase = k + 1
                if k < MAX_PASSES:
                    for g in range(NG):
                        free = None
                        if g >= 2:
                            free = (mixed, nth("mixed", phase, g - 2)) if k == 0 else \
                                (projected, nth("projected", phase, g - 2))
                        copy_transposed(phase, g, agg_t[:, g % 2, :], free)
                        if k == 0:
                            if g == 0:
                                sc.wait_ge(params_in, PARAMS)
                            sc.wait_ge(mixed, nth("mixed", phase, g))
                            n = (GROUPS[g][1] - GROUPS[g][0]) * P
                            sc.activation(feat[:, span(g)], ps_f[g % 2][:, 0:n], ACT.Tanh,
                                          bias=COL["out1"]).then_inc(activated, 1)
                        else:
                            sc.wait_ge(ln_var, g + 2)
                            t0, t1 = 2 * GROUPS[g][0], 2 * GROUPS[g][1]
                            sc.activation(stat[:, 3, t0:t1], stat[:, 2, t0:t1], ACT.Sqrt).then_inc(ln_root, 1)
                else:
                    i = k - MAX_PASSES
                    for g in range(NG):
                        copy_transposed(phase, g, agg_t[:, g % 2, :],
                                        (mixed, nth("mixed", phase, g - 2)) if g >= 2 else None)
                        sc.wait_ge(mixed, nth("mixed", phase, g))
                        n = (GROUPS[g][1] - GROUPS[g][0]) * P
                        sc.activation(feat[:, span(g)], ps_f[g % 2][:, 0:n], ACT.Identity,
                                      bias=COL[f"b1_{i}"]).then_inc(activated, 1)
                    sc.wait_ge(bn_in, 3 * i + 3)
                    sc.activation(bn_std[:, :], bn_var[:, :], ACT.Sqrt).then_inc(bn_root, 1)
                    sc.wait_ge(bn_ready, i + 1)
                    for g in range(NG):
                        sc.activation(feat[:, span(g)], feat[:, span(g)], ACT.Relu, bias=bn_shift[:, :],
                                      scale=bn_scale[:, :]).then_inc(normed, 1)

        @block.vector
        def _(v):
            owned = [0]

            def then(instruction):
                owned[0] += 1
                instruction.then_inc(own, 1)
                v.wait_ge(own, owned[0])

            v.memset(x_res[:, LAST_ROWS * D:], 0.0).then_inc(zeroed, 1)
            v.memset(dst[0:1, 0:1 + PADS], -1).then_inc(zeroed, 1)
            v.memset(src[0:1, 0:PADS], 0).then_inc(zeroed, 1)
            v.memset(weight[0:1, 0:PADS], 0.0).then_inc(zeroed, 1)
            v.memset(zeros[:, :], 0.0).then_inc(zeroed, 1)
            v.memset(carry[:, :, :], 0.0).then_inc(zeroed, 1)
            v.memset(ones[:, :], 1.0).then_inc(zeroed, 1)
            v.memset(w_all[:, :, :], 0.0).then_inc(zeroed, 1)
            v.memset(bias_ones[:, :], 1.0).then_inc(zeroed, 1)
            v.memset(bias_f, 0.0).then_inc(zeroed, 1)
            v.memset(bias_parts[:, :], 0.0).then_inc(zeroed, 1)

            v.wait_ge(x_in, 48)
            then(v.tensor_reduce(stat[:, 0, :], by_tile(x_res[:, :]), AX.X, ALU.add))
            then(v.tensor_scalar(stat[:, 1, :], stat[:, 0, :], -1.0 / D, None, ALU.mult))
            v.tensor_tensor(by_tile(node[:, :]), by_tile(x_res[:, :]),
                            stat[:, 1, :, None].broadcast_to([P, NT, D]), ALU.add).then_inc(ln_centred, 1)
            v.wait_ge(sample_in, 16)
            v.tensor_copy(sample_f, sample_i).then_inc(sample_ready, 1)
            v.wait_ge(ln_squared, 1)
            then(v.tensor_reduce(stat[:, 0, :], by_tile(feat[:, :]), AX.X, ALU.add))
            v.tensor_scalar(stat[:, 2, :], stat[:, 0, :], 1.0 / D, LN_EPS, ALU.mult, ALU.add).then_inc(ln_var, 1)
            v.wait_ge(ln_root, 1)
            then(v.reciprocal(stat[:, 0, :], stat[:, 3, :]))
            v.scalar_tensor_tensor(by_tile(node[:, :]), by_tile(node[:, :]), 0.0,
                                   stat[:, 0, :, None].broadcast_to([P, NT, D]), ALU.max, ALU.mult).then_inc(ln_ready, 1)

            v.wait_ge(biases_in, 16 * len(ROWS_FROM))
            v.wait_ge(zeroed, 11)
            rest = bias_f
            for n, at in enumerate(PART_AT):
                then(v.tensor_copy(bias_split[n], rest))
                if n < len(PART_AT) - 1:
                    then(v.tensor_tensor(bias_rest, rest, bias_split[n], ALU.subtract))
                    rest = bias_rest
                v.tensor_copy(bias_parts[at:at + 1, :], bias_split[n][at:at + 1, :]).then_inc(biases_ready, 1)

            v.wait_ge(edges_in, 16 * 10)
            v.wait_ge(zeroed, 6)
            for r in (A, B):
                n = REGION_STEPS[r]
                v.tensor_tensor(same[:, FIRST_COL[r]:FIRST_COL[r] + n], dst_at[r][:, 1:n + 1], dst_at[r][:, 0:n],
                                ALU.is_equal).then_inc(same_ready, 1)

            def emit_relu(phase, g):
                v.wait_ge(projected, nth("projected", phase, g))
                n = (GROUPS[g][1] - GROUPS[g][0]) * P
                v.tensor_scalar(node[:, span(g)], ps_m[g % 2][:, 0:n], 0.0, None, ALU.max).then_inc(emitted, 1)

            for g in range(NG):
                emit_relu(0, g)

            def start_search():
                for r in (A, B):
                    n = REGION_STEPS[r]
                    then(v.tensor_tensor(lead_flags[:, 0:n], dst_at[r][:, 1:n + 1], dst_at[r][:, 0:1].broadcast_to([P, n]),
                                         ALU.is_equal))
                    then(v.tensor_reduce(lead[:, r:r + 1], lead_flags[:, 0:n], AX.X, ALU.add))
                    v.tensor_scalar(whole[:, r:r + 1], lead[:, r:r + 1], float(n), None, ALU.is_equal).then_inc(lead_ready, 1)
                v.wait_ge(table_in, 16 * TABLE_DMAS)
                v.memset(scatter_src[0:1, 0:PADS], 0).then_inc(lead_ready, 1)
                then(v.tensor_scalar(cont[:, :], lead[:, :], 0.0, None, ALU.is_gt))
                v.wait_ge(consts, 5)
                then(v.tensor_copy(fix_f[:, :], base_i[:, :]))
                then(v.tensor_scalar(lead[:, :], lead[:, :], -1.0, 0.0, ALU.add, ALU.max))
                then(v.tensor_tensor(fix_row[:, :], fix_f[:, :], lead[:, :], ALU.add))
                v.wait_ge(samples_ps, 1)
                for h, bank in enumerate(ps_f):
                    then(v.tensor_copy(samples[:, h * HALF_SAMPLES:(h + 1) * HALF_SAMPLES], bank[:, 0:HALF_SAMPLES]))
                v.wait_ge(whole_ps, 1)
                then(v.tensor_copy(whole_t[:, :, :], ps_tail[0:D, 0:2 * P].rearrange("p (r n) -> p r n", r=2)))
                v.tensor_copy(nval[:, :], nval_i[:, :]).then_inc(tile_counted, 1)

            def count_tiles(turn):
                for c in range(SEARCH_TILES):
                    t = bass.ds(turn * SEARCH_TILES + (c - SEARCH_TILES), 1)
                    v.wait_ge(tile_counted, turn * SEARCH_TILES + (c - SEARCH_TILES + 1))
                    v.tensor_scalar(row_flags, samples[:, :], nval[:, t], None, ALU.is_le, ALU.add,
                                    accum_out=cnt_rows[:, t]).then_inc(tile_counted, 1)

            def ask_rows():
                v.wait_ge(tile_counted, NT + 2)
                then(v.tensor_scalar(cnt_rows[:, :], cnt_rows[:, :], float(E_ROWS - 1), None, ALU.min))
                v.tensor_copy(row_idx[:, :], cnt_rows[:, :]).then_inc(row_wanted, 1)

            def finish_search():
                for t in range(NT + 1):
                    v.wait_ge(row_f, t + 1)
                    v.tensor_scalar(search_flags, search_f[:, t % SEARCH_SLOTS, :],
                                    nval[:, t:t + 1], None, ALU.is_le, ALU.add,
                                    accum_out=cnt_in[:, t:t + 1]).then_inc(row_counted, 1)
                    v.wait_ge(row_counted, t + 1)
                then(v.scalar_tensor_tensor(cnt[:, :], cnt_rows[:, :], float(ROW), cnt_in[:, :], ALU.mult, ALU.add))
                then(v.tensor_tensor(some[:, :], cnt[:, 1:NT + 1], cnt[:, 0:NT], ALU.is_gt))
                then(v.scalar_tensor_tensor(ends_f[:, :], cnt[:, 1:NT + 1], float(PADS - 1 - ZERO_ROW), some[:, :],
                                            ALU.add, ALU.mult))
                then(v.tensor_scalar(ends_f[:, :], ends_f[:, :], float(ZERO_ROW), None, ALU.add))
                then(v.tensor_copy(ends[:, :], ends_f[:, :]))
                then(v.tensor_tensor(in_b[:, :], cnt[:, 1:NT + 1], cnt[:, 0:NT], ALU.subtract))
                then(v.tensor_reduce(guard[:, 0:1], in_b[:, :], AX.X, ALU.max))
                v.tensor_copy(guard[:, 1:2], cnt[:, NT:NT + 1]).then_inc(guard_ready, 1)
                v.wait_ge(guard_ps, 1)
                then(v.tensor_reduce(guard_row[:, 0:1], ps_tail[0:1, 0:P], AX.X, ALU.max))
                then(v.tensor_scalar(guard_row[:, 0:1], guard_row[:, 0:1], float(MAX_DEGREE), None, ALU.is_gt))
                for n, (p, edges, fails) in enumerate((
                        (DENSE_TO[0], PART_EDGES, ALU.is_lt), (DENSE_FROM[1], PART_EDGES, ALU.is_gt),
                        (DENSE_TO[1], EDGES_A, ALU.is_lt), (LOW, EDGES_A, ALU.is_gt))):
                    then(v.tensor_scalar(guard_row[:, n + 1:n + 2], ps_tail[0:1, P + p - 1:P + p], float(edges), None, fails))
                then(v.tensor_reduce(general_f[:, :], guard_row[:, 0:5], AX.X, ALU.max))
                v.tensor_copy(general_i[:, :], general_f[:, :]).then_inc(flag_ready, 1)
                v.wait_ge(guard_ps, 2)
                then(v.tensor_scalar(dense_f[:, :], ps_bn[:, 0:1], -1.0, 1.0, ALU.mult, ALU.add))
                then(v.tensor_scalar(in_b[:, :], ends_f[:, :], float(FIRST_ROW[B]), dense_f[:, :], ALU.is_lt, ALU.mult))
                then(v.tensor_scalar(some[:, :], ends_f[:, :], -1.0, float(ZERO_ROW), ALU.mult, ALU.add))
                then(v.tensor_tensor(some[:, :], some[:, :], in_b[:, :], ALU.mult))
                then(v.tensor_tensor(ends_b[:, :, :].rearrange("p h q -> p q h"), ends_f[:, :].rearrange("p (q h) -> p q h", h=2),
                                     some[:, :].rearrange("p (q h) -> p q h", h=2), ALU.add))
                then(v.tensor_scalar(low_mask[:, :], nval[:, 0:1], float(LOW * NT - 1), None, ALU.is_lt))
                then(v.tensor_scalar(some[:, :], ends_f[:, :], -float(ZERO_ROW), low_mask[:, :], ALU.add, ALU.mult))
                v.tensor_scalar(ends_low[:, :], some[:, :], float(ZERO_ROW), None, ALU.add).then_inc(ends_ready, 1)

            last_state = state[:, SLOTS - 1, SLOT_STEPS - 1, :]

            def scatter_elements():
                p_part = idx_hi
                off = scatter_idx.bitcast(F32)
                v.wait_ge(parts_in, 16 * 8)
                then(v.tensor_scalar(p_part, scatter_idx, 1.0 / NT, 0.5 / NT - 0.5, ALU.mult, ALU.add))
                then(v.scalar_tensor_tensor(t_part, p_part, -float(NT), scatter_idx, ALU.mult, ALU.add))
                then(v.tensor_scalar(off, t_part, 0.0, None, ALU.is_lt))
                then(v.tensor_tensor(p_part, p_part, off, ALU.subtract))
                then(v.scalar_tensor_tensor(t_part, off, float(NT), t_part, ALU.mult, ALU.add))
                then(v.tensor_scalar(off, t_part, float(NT), None, ALU.is_ge))
                then(v.tensor_tensor(p_part, p_part, off, ALU.add))
                then(v.scalar_tensor_tensor(t_part, off, -float(NT), t_part, ALU.mult, ALU.add))
                for h in range(2):
                    part = slice(h * PART_STEPS, (h + 1) * PART_STEPS)
                    if DENSE_FROM[h]:
                        then(v.tensor_scalar(p_part[:, part], p_part[:, part], -float(DENSE_FROM[h]), None, ALU.add))
                    then(v.scalar_tensor_tensor(scatter_idx[:, part], t_part[:, part], float(DENSE_P[h]), p_part[:, part],
                                                ALU.mult, ALU.add))
                    then(v.tensor_scalar(idx_hi[:, part], scatter_src[:, part], float(DENSE[h] >> DENSE_SHIFT), None, ALU.mult))
                v.tensor_scalar(idx_hi, idx_hi, DENSE_SHIFT, None, ALU.logical_shift_left).then_inc(cols_ready, 1)

            def fold_region(k, r):
                weighs = k >= MAX_PASSES
                op = ALU.add if weighs else ALU.max
                turns, steps = TURNS[r], REGION_STEPS[r]
                landed = TURNS[B] if r == A else 0

                def fold_turn(turn, first):
                    for s in range(SLOTS):
                        half, at = divmod(s * SLOT_STEPS, HALF)
                        v.wait_ge(gathered[k][s], turn * (16 * SLOT_STEPS) + 16 * SLOT_STEPS * (landed + 1))
                        if at == 0:
                            v.wait_ge(same_staged[r], turn * 2 + (k * 2 * turns + half + 1))
                            if weighs:
                                v.wait_ge(weight_staged[r], turn * 2 + ((k - MAX_PASSES) * 2 * turns + half + 1))
                        if weighs:
                            w = weight_st[:, s * SLOT_STEPS:(s + 1) * SLOT_STEPS]
                            v.tensor_tensor(rows[:, s, :, :], rows[:, s, :, :],
                                            w[:, :, None].broadcast_to([P, SLOT_STEPS, D]), ALU.mult).then_inc(weighted[r], 1)
                            v.wait_ge(weighted[r], turn * SLOTS + ((k - MAX_PASSES) * SLOTS * turns + s + 1))
                        if not first:
                            v.wait_ge(stored[r][s], turn * 16 + 16 * turns * k)
                        elif r == A:
                            v.wait_ge(stored[B][s], 16 * TURNS[B] * (k + 1))
                        for i in range(SLOT_STEPS):
                            j = s * SLOT_STEPS + i
                            before = state[:, s, i - 1, :] if i else state[:, (s - 1) % SLOTS, SLOT_STEPS - 1, :]
                            if first and j == 0:
                                before = zeros[:, 0:D]
                            else:
                                v.wait_ge(step_done[r], turn * TURN + (k * steps + j))
                            v.scalar_tensor_tensor(state[:, s, i, :], before, same_st[:, j:j + 1], rows[:, s, i, :],
                                                   ALU.mult, op).then_inc(step_done[r], 1)

                fold_turn(0, True)
                rest = 1
                if k == 0 and r == B:
                    rest = 1 + SEARCH_TURNS
                    start_search()
                    with v.Fori(1, rest) as turn:
                        fold_turn(turn, False)
                        count_tiles(turn)
                    ask_rows()
                with v.Fori(rest, turns) as turn:
                    fold_turn(turn, False)
                v.wait_ge(step_done[r], (k + 1) * steps)
                v.tensor_copy(finals[:, r, :], last_state).then_inc(final_ready[r], 1)
                v.wait_ge(final_ready[r], k + 1)

            def fix_region(k, r):
                op = ALU.add if k >= MAX_PASSES else ALU.max
                before = 0.0 if r == A else carry[:, A, P:P + 1]
                if r == B:
                    then(v.tensor_copy(carry[:, B, 0:1], carry[:, A, P:P + 1]))
                v.wait_ge(tail_t[r], k + 1)
                v.tensor_tensor_scan(carry[:, r, 1:P + 1], whole_t[:, r, :], ps_tail[0:D, r * P:(r + 1) * P], before,
                                     ALU.mult, op).then_inc(carried[r], 1)
                v.wait_ge(carry_t[r], k + 1)
                v.wait_ge(fix_in[r], 16 * (k + 1))
                v.scalar_tensor_tensor(fixed_rows[:, r, :], ps_carry[r], cont[:, r:r + 1], fixed_rows[:, r, :],
                                       ALU.mult, op).then_inc(fixed[r], 1)
                v.wait_ge(carried[r], k + 1)

            for k in range(PASSES):
                if k == MAX_PASSES:
                    general = flag(v)
                    with v.If(general == 0):
                        v.memset(carry[:, A, P:P + 1], 0.0).then_inc(carry_set, 1)
                    with v.Else():
                        v.memset(bn_dev[:, :], 0.0).then_inc(carry_set, 1)
                    v.wait_ge(carry_set, 1)
                fold_region(k, B)
                if k == 0:
                    finish_search()
                    scatter_elements()
                if k < MAX_PASSES:
                    fold_region(k, A)
                    fix_region(k, A)
                else:
                    with v.If(general == 1):
                        fold_region(k, A)
                        fix_region(k, A)
                    v.nop()
                fix_region(k, B)

                phase = k + 1
                if k == 0:
                    for g in range(NG):
                        emit_relu(phase, g)
                elif k == 1:
                    for g in range(NG):
                        a, b = GROUPS[g]
                        t0, t1, n = 2 * a, 2 * b, (b - a) * P
                        v.wait_ge(projected, nth("projected", phase, g))
                        then(v.tensor_tensor(x_res[:, span(g)], x_res[:, span(g)], ps_m[g % 2][:, 0:n], ALU.add))
                        then(v.tensor_reduce(stat[:, 0, t0:t1], by_tile(x_res[:, span(g)]), AX.X, ALU.add))
                        then(v.tensor_scalar(stat[:, 1, t0:t1], stat[:, 0, t0:t1], -1.0 / D, None, ALU.mult))
                        then(v.tensor_tensor(by_tile(centred[:, 0:n]), by_tile(x_res[:, span(g)]),
                                             stat[:, 1, t0:t1, None].broadcast_to([P, t1 - t0, D]), ALU.add))
                        then(v.tensor_tensor(squares[:, 0:n], centred[:, 0:n], centred[:, 0:n], ALU.mult))
                        then(v.tensor_reduce(stat[:, 0, t0:t1], by_tile(squares[:, 0:n]), AX.X, ALU.add))
                        v.tensor_scalar(stat[:, 2, t0:t1], stat[:, 0, t0:t1], 1.0 / D, LN_EPS,
                                        ALU.mult, ALU.add).then_inc(ln_var, 1)
                        v.wait_ge(ln_root, g + 2)
                        then(v.reciprocal(stat[:, 0, t0:t1], stat[:, 3, t0:t1]))
                        v.scalar_tensor_tensor(by_tile(node[:, span(g)]), by_tile(centred[:, 0:n]), 0.0,
                                               stat[:, 0, t0:t1, None].broadcast_to([P, t1 - t0, D]),
                                               ALU.max, ALU.mult).then_inc(emitted, 1)
                        v.wait_ge(emitted, nth("emitted", phase, g))
                else:
                    i = k - MAX_PASSES

                    def pair_stats(g):
                        v.wait_ge(activated, nth("activated", phase, g))
                        for q in range(*GROUPS[g]):
                            real = P if 2 * q < LAST_ROWS else P - 1
                            last = v.bn_stats(bn[:, q, :], feat[:, q * P:q * P + real])
                        return last

                    def add_dense(g):
                        a, b = GROUPS[g]
                        v.wait_ge(dense_out, CHUNKS * (i + 1))
                        v.wait_ge(copied, nth("copied", phase, g))
                        to = tiles_of(agg_t[:, g % 2, 0:(b - a) * P])
                        v.tensor_tensor(to, to, tiles_of(feat[:, span(g)]), ALU.add).then_inc(dense_added, 1)

                    for g in range(NG):
                        add_dense(g)
                        if g >= 1:
                            pair_stats(g - 1)
                    then(pair_stats(NG - 1))
                    v.bn_aggr(bn_mv[:, :], bn[:, :, :].rearrange("p q s -> p (q s)")).then_inc(bn_in, 1)
                    v.wait_ge(bn_ps, 2 * i + 1)
                    then(v.tensor_copy(bn_mean[:, :], ps_bn[:, 0:1]))
                    then(v.tensor_tensor(bn_dev[:, :], bn_mv[:, 0:1], bn_mean[:, :], ALU.subtract))
                    then(v.tensor_tensor(bn_dev[:, :], bn_dev[:, :], bn_dev[:, :], ALU.mult))
                    v.tensor_tensor(bn_dev[:, :], bn_dev[:, :], bn_mv[:, 1:2], ALU.add).then_inc(bn_in, 1)
                    v.wait_ge(bn_ps, 2 * i + 2)
                    v.tensor_scalar(bn_var[:, :], ps_bn[:, 1:2], BN_EPS, None, ALU.add).then_inc(bn_in, 1)
                    v.wait_ge(bn_root, i + 1)
                    then(v.reciprocal(bn_dev[:, :], bn_std[:, :]))
                    then(v.tensor_tensor(bn_scale[:, :], bn_dev[:, :], COL[f"gamma_{i}"], ALU.mult))
                    then(v.tensor_tensor(bn_mean[:, :], bn_mean[:, :], bn_scale[:, :], ALU.mult))
                    v.tensor_tensor(bn_shift[:, :], COL[f"beta_{i}"], bn_mean[:, :], ALU.subtract).then_inc(bn_ready, 1)
                    for g in range(NG):
                        if k < PASSES - 1:
                            emit_relu(phase, g)
                        else:
                            v.wait_ge(projected, nth("projected", phase, g))
                            n = (GROUPS[g][1] - GROUPS[g][0]) * P
                            v.scalar_tensor_tensor(node[:, span(g)], ps_m[g % 2][:, 0:n], 0.0, x_res[:, span(g)],
                                                   ALU.max, ALU.add).then_inc(emitted, 1)

        @block.tensor
        def _(pe):
            def transpose_group(phase, g, of, ready):
                pe.wait_ge(*ready)
                n = nth("transposed", phase, g)
                if n > 2:
                    pe.wait_ge(copied, n - 2)
                a, b = GROUPS[g]
                for q in range(a, b):
                    last = pe.transpose(ps_t[g % 2][:, (q - a) * P:(q - a + 1) * P], of[:, q * P:(q + 1) * P], ident[:, :])
                last.then_inc(transposed, 1)

            def place_group(phase, g):
                pe.wait_ge(agg_in[g], agg_landed(phase - 1, g))
                pe.wait_ge(copied, nth("transposed", phase, g) - 2)
                a, b = GROUPS[g]
                for q in range(a, b):
                    to = ps_t[g % 2][:, (q - a) * P:(q - a + 1) * P]
                    pair = node[:, q * P:(q + 1) * P]
                    for h in range(2):
                        pe.matmul(to[h * D:(h + 1) * D, LOW:P], agg[0:2 * HIGH, q * D:(q + 1) * D],
                                  ident[0:2 * HIGH, h * HIGH:(h + 1) * HIGH], start=True, stop=False)
                    pe.matmul(to[:, LOW:P], pair, ident[:, LOW:P], start=False, stop=True)
                    last = pe.matmul(to[:, 0:LOW], pair, ident[:, 0:LOW], start=True, stop=True)
                last.then_inc(transposed, 1)

            def bank_free(phase, g):
                n = nth("projected", phase, g)
                if n > 2:
                    pe.wait_ge(emitted, n - 2)

            def project(phase, g, bias, parts):
                a, b = GROUPS[g]
                n = (b - a) * P
                pe.matmul(ps_m[g % 2][:, 0:n], bias_ones[:, :], bias.broadcast_to([PARTS, n // D, D]), start=True, stop=False)
                for q in range(a, b):
                    for m, (of, w) in enumerate(parts):
                        last = pe.matmul(ps_m[g % 2][:, (q - a) * P:(q - a + 1) * P],
                                         of[:, (q - a) * P:(q - a + 1) * P], w, start=False,
                                         stop=q == b - 1 and m == len(parts) - 1)
                last.then_inc(projected, 1)

            pe.wait_ge(consts, 9)
            pe.wait_ge(zeroed, 9)
            pe.wait_ge(biases_ready, len(PART_AT))
            pe.wait_ge(params_in, PARAMS)
            for g in range(NG + 1):
                if g < NG:
                    transpose_group(0, g, node, (ln_ready, 1))
                if g >= 1:
                    pe.wait_ge(copied, nth("copied", 0, g - 1))
                    bank_free(0, g - 1)
                    project(0, g - 1, B_ROW["pool1"], [(feat[:, span(g - 1)], W["pool1"])])
            pe.wait_ge(sample_ready, 1)
            for h, bank in enumerate(ps_f):
                last = pe.matmul(bank[:, 0:HALF_SAMPLES], ones[:, :], sample_f[0:1, h * HALF_SAMPLES:(h + 1) * HALF_SAMPLES],
                                 start=True, stop=True)
            last.then_inc(samples_ps, 1)
            pe.wait_ge(lead_ready, 2)
            for r in (A, B):
                last = pe.matmul(ps_tail[0:D, r * P:(r + 1) * P], whole[:, r:r + 1].broadcast_to([P, D]), ident[:, :],
                                 start=True, stop=True)
            last.then_inc(whole_ps, 1)
            pe.wait_ge(guard_ready, 1)
            for n in range(2):
                last = pe.transpose(ps_tail[0:1, n * P:(n + 1) * P], guard[:, n:n + 1], ident[:, :])
            last.then_inc(guard_ps, 1)
            pe.wait_ge(flag_ready, 1)
            pe.matmul(ps_bn[:, 0:1], ones[:, :], general_f[:, :], start=True, stop=True).then_inc(guard_ps, 1)

            def fix_region(k, r):
                pe.wait_ge(final_ready[r], k + 1)
                pe.transpose(ps_tail[0:D, r * P:(r + 1) * P], finals[:, r, :], ident[:, :]).then_inc(tail_t[r], 1)
                pe.wait_ge(carried[r], k + 1)
                pe.transpose(ps_carry[r], carry[:, r, 0:P], ident[0:D, 0:D]).then_inc(carry_t[r], 1)
                pe.wait_ge(fixed[r], k + 1)

            def dense_sums(k):
                i = k - MAX_PASSES

                def add_zeros(start):
                    for bank in ps_dense:
                        last = pe.matmul(bank[:, 0:BANK], zeros[:, 0:P], zeros[:, 0:BANK], start=start, stop=not start)
                    return last

                def source_tiles(turn, first):
                    for u in range(DENSE_TILES):
                        pe.wait_ge(x_tile_in[u], turn * 16 + 16 * (i * (NT // DENSE_TILES) + 1))
                        if first and u == 0:
                            add_zeros(True)
                        for c in range(CHUNKS):
                            pe.wait_ge(chunk_in[c], turn * (32 * DENSE_TILES) + 32 * (i * NT + u + 1))
                            for part in range(2):
                                for h in range(2):
                                    columns = chunk[:, c, CHUNK_AT[part]:CHUNK_AT[part] + CHUNK[part]].rearrange(
                                        "p (q h m) -> p h q m", h=2, m=DENSE_P[part])
                                    to = ps_dense[c][h * D:(h + 1) * D, 0:BANK].rearrange("p (q n) -> p q n", n=DENSE_WIDTH)
                                    mm = pe.matmul(to[:, :, DENSE_FROM[part]:DENSE_TO[part]], x_tile[:, u, :],
                                                   columns[:, h, :, :], start=False, stop=False)
                            mm.then_inc(chunk_used, 1)

                source_tiles(0, True)
                with pe.Fori(1, NT // DENSE_TILES) as turn:
                    source_tiles(turn, False)
                add_zeros(False).then_inc(dense_summed, 1)

            def low_sums(k):
                pe.wait_ge(low_in, 16 * NT * (k - MAX_PASSES + 1))
                for q in range(PAIRS):
                    c, at = divmod(q, CHUNK_PAIRS)
                    last = pe.matmul(ps_dense[c][:, at * DENSE_WIDTH:(at + 1) * DENSE_WIDTH], agg[:, q * P:(q + 1) * P],
                                     ident[:, 0:DENSE_WIDTH], start=True, stop=True)
                last.then_inc(dense_summed, 1)

            general = flag(pe)
            for k in range(PASSES):
                if k < MAX_PASSES:
                    fix_region(k, A)
                else:
                    with pe.If(general == 1):
                        fix_region(k, A)
                    with pe.Else():
                        dense_sums(k)
                    pe.nop()
                fix_region(k, B)
                if k >= MAX_PASSES:
                    with pe.If(general == 1):
                        low_sums(k)
                    pe.nop()
                    pe.wait_ge(dense_out, CHUNKS * (k - MAX_PASSES + 1))

                phase = k + 1
                if k == 0:
                    for g in range(NG + 2):
                        if g < NG:
                            transpose_group(phase, g, agg, (agg_in[g], agg_landed(k, g)))
                        if 1 <= g <= NG:
                            c = g - 1
                            n = (GROUPS[c][1] - GROUPS[c][0]) * P
                            pe.wait_ge(copied, nth("copied", phase, c))
                            if c >= 2:
                                pe.wait_ge(activated, nth("activated", phase, c - 2))
                            pe.matmul(ps_f[c % 2][:, 0:n], W["self1"], feat[:, span(c)], start=True, stop=False)
                            pe.matmul(ps_f[c % 2][:, 0:n], W["neigh1"], agg_t[:, c % 2, 0:n], start=False,
                                      stop=True).then_inc(mixed, 1)
                        if g >= 2:
                            c = g - 2
                            pe.wait_ge(activated, nth("activated", phase, c))
                            bank_free(phase, c)
                            project(phase, c, B_ROW["pool2"], [(feat[:, span(c)], W["pool2"])])
                elif k == 1:
                    for g in range(NG + 1):
                        if g < NG:
                            transpose_group(phase, g, agg, (agg_in[g], agg_landed(k, g)))
                        if g >= 1:
                            c = g - 1
                            pe.wait_ge(copied, nth("copied", phase, c))
                            bank_free(phase, c)
                            project(phase, c, B_ROW["out2"],
                                    [(feat[:, span(c)], W["self2"]), (agg_t[:, c % 2, :], W["neigh2"])])
                else:
                    i = k - MAX_PASSES
                    for g in range(NG + 1):
                        if g < NG:
                            place_group(phase, g)
                        if g >= 1:
                            c = g - 1
                            n = (GROUPS[c][1] - GROUPS[c][0]) * P
                            pe.wait_ge(dense_added, nth("dense_added", phase, c))
                            if nth("mixed", phase, c) > 2:
                                pe.wait_ge(activated, nth("activated", phase, c) - 2)
                            pe.matmul(ps_f[c % 2][:, 0:n], W[f"w1_{i}"], agg_t[:, c % 2, 0:n], start=True,
                                      stop=True).then_inc(mixed, 1)
                    pe.wait_ge(bn_in, 3 * i + 1)
                    pe.matmul(ps_bn[:, 0:1], fold[:, :], bn_mv[:, 0:1], start=True, stop=True).then_inc(bn_ps, 1)
                    pe.wait_ge(bn_in, 3 * i + 2)
                    pe.matmul(ps_bn[:, 1:2], fold[:, :], bn_dev[:, :], start=True, stop=True).then_inc(bn_ps, 1)
                    for g in range(NG):
                        pe.wait_ge(normed, nth("normed", phase, g))
                        bank_free(phase, g)
                        project(phase, g, B_ROW[f"b2_{i}"], [(feat[:, span(g)], W[f"w2_{i}"])])


_INS = ["x", "src", "dst", "edge_weight1",
        "L0_gnn_W_pool1", "L0_gnn_b_pool1", "L0_gnn_W_self1", "L0_gnn_W_neigh1", "L0_gnn_bias1",
        "L0_gnn_W_pool2", "L0_gnn_b_pool2", "L0_gnn_W_self2", "L0_gnn_W_neigh2", "L0_gnn_bias2",
        "L1_gnn_W1", "L1_gnn_b1", "L1_gnn_gamma", "L1_gnn_beta", "L1_gnn_W2", "L1_gnn_b2"]


def kernel(**inputs):
    import concourse.bacc as bacc
    from concourse.bass_utils import run_bass_kernel_spmd

    nc = bacc.Bacc("TRN2", target_bir_lowering=False, num_devices=1)
    arrays, io = {}, {}
    for name in _INS:
        a = np.ascontiguousarray(inputs[name])
        if name == "edge_weight1":
            a = a.reshape(-1)
        arrays[f"in_{name}"] = a
        io[name] = nc.dram_tensor(f"in_{name}", a.shape, mybir.dt.from_np(a.dtype), kind="ExternalInput").ap()
    io["out"] = nc.dram_tensor("out", [N, D], mybir.dt.float32, kind="ExternalOutput").ap()
    build(nc, io)
    r = run_bass_kernel_spmd(nc, [arrays], core_ids=[0])
    return r.results[0]["out"]
```
